# Optimizing a Trainium2 kernel written in Bass

```python
import numpy as np
import jax
import jax.numpy as jnp

def _softmax(x, axis=-1):
    return jax.nn.softmax(x, axis=axis)

def _gelu(x):
    return jax.nn.gelu(x, approximate=True)

def _silu(x):
    return jax.nn.silu(x)

def _sigmoid(x):
    return jax.nn.sigmoid(x)

def _layernorm(x, axis=-1, eps=1e-05):
    m = jnp.mean(x, axis=axis, keepdims=True)
    v = jnp.var(x, axis=axis, keepdims=True)
    return (x - m) / jnp.sqrt(v + eps)

def _scatter_add(tgt, idx, src, axis=0):
    return tgt.at[idx].add(src)

def _segment_sum(src, seg, n):
    return jax.ops.segment_sum(src, seg, n)
kernel_name = 'mk_adj_resnorm_d2_adj_r2_4db42d'

def setup_inputs(seed: int=0):
    np.random.seed(seed)
    _w = jnp.asarray

    def _rec_inputs():
        import jax
        import jax.numpy as jnp
        _gk = jax.random.key(seed)
        x = -0.0002928 + 1 * jax.random.normal(jax.random.fold_in(_gk, 1), (4096, 256), jnp.float32)
        _w = (1.0 + jnp.arange(4096, dtype=jnp.float32)) ** (-0.5)
        _w = _w / _w.mean()
        _pij = jnp.clip(0.00195312 * _w[:, None] * _w[None, :], 0.0, 1.0)
        _a = jax.random.uniform(jax.random.fold_in(_gk, 2), (4096, 4096)) < _pij
        adj = _a.astype(jnp.int32)
        return (x, adj)
    x, adj = _rec_inputs()

    def _L0_gnn_setup():
        import jax, jax.numpy as jnp
        import numpy as np
        EPS = 1e-08
        key = jax.random.key(seed)
        k1, k2, k3 = jax.random.split(key, 3)
        N, IN_DIM, OUT_DIM = (4096, 256, 256)
        h = jax.random.normal(k1, (N, IN_DIM), dtype=jnp.float32)
        adj = jax.random.randint(k2, (N, N), 0, 2, dtype=jnp.int32)
        W = jax.random.normal(k3, (OUT_DIM, IN_DIM), dtype=jnp.float32) * (1.0 / np.sqrt(IN_DIM))
        return {'h': h, 'adj': adj, 'W': W}
    _L0_gnn_all = _L0_gnn_setup()
    _L0_gnn_in = {k: v for k, v in _L0_gnn_all.items() if k in ('W',)}
    del _L0_gnn_all

    def _L1_gnn_setup():
        import jax, jax.numpy as jnp
        import numpy as np
        N, D_IN, D_OUT = (4096, 256, 256)
        key = jax.random.key(seed)
        ks = jax.random.split(key, 8)
        scale_in = 1.0 / np.sqrt(D_IN)
        scale_cat = 1.0 / np.sqrt(2 * D_OUT)
        return {'x': jax.random.normal(ks[0], (N, D_IN), dtype=jnp.float32), 'adj': jax.random.randint(ks[1], (N, N), 0, 2, dtype=jnp.int32), 'W_self': jax.random.uniform(ks[2], (D_IN, D_OUT), jnp.float32, -scale_in, scale_in), 'b_self': jax.random.uniform(ks[3], (D_OUT,), jnp.float32, -scale_in, scale_in), 'W_nb': jax.random.uniform(ks[4], (D_IN, D_OUT), jnp.float32, -scale_in, scale_in), 'b_nb': jax.random.uniform(ks[5], (D_OUT,), jnp.float32, -scale_in, scale_in), 'W_comb': jax.random.uniform(ks[6], (2 * D_OUT, D_OUT), jnp.float32, -scale_cat, scale_cat), 'b_comb': jax.random.uniform(ks[7], (D_OUT,), jnp.float32, -scale_cat, scale_cat)}
    _L1_gnn_all = _L1_gnn_setup()
    _L1_gnn_in = {k: v for k, v in _L1_gnn_all.items() if k in ('W_self', 'b_self', 'W_nb', 'b_nb', 'W_comb', 'b_comb')}
    del _L1_gnn_all
    return {'x': x, 'adj': adj, 'L0_gnn_W': _L0_gnn_in['W'], 'L1_gnn_W_self': _L1_gnn_in['W_self'], 'L1_gnn_b_self': _L1_gnn_in['b_self'], 'L1_gnn_W_nb': _L1_gnn_in['W_nb'], 'L1_gnn_b_nb': _L1_gnn_in['b_nb'], 'L1_gnn_W_comb': _L1_gnn_in['W_comb'], 'L1_gnn_b_comb': _L1_gnn_in['b_comb']}

def reference(x, adj, L0_gnn_W, L1_gnn_W_self, L1_gnn_b_self, L1_gnn_W_nb, L1_gnn_b_nb, L1_gnn_W_comb, L1_gnn_b_comb):
    import jax
    import jax.numpy as jnp

    def _L0_gnn_ref(h, adj, W):
        import jax, jax.numpy as jnp
        import numpy as np
        EPS = 1e-08
        Wh = h @ W.T
        N = Wh.shape[0]
        norms = jnp.linalg.norm(Wh, axis=1, keepdims=True)
        sim = Wh @ Wh.T / (norms * norms.T + EPS)
        mask = (adj > 0) | jnp.eye(N, dtype=bool)
        sim_masked = jnp.where(mask, sim, -jnp.inf)
        alpha = jax.nn.softmax(sim_masked, axis=1)
        return alpha @ Wh

    def _L1_gnn_ref(x, adj, W_self, b_self, W_nb, b_nb, W_comb, b_comb):
        import jax, jax.numpy as jnp
        import numpy as np
        N, D_IN, D_OUT = (4096, 256, 256)
        mask = (adj > 0).astype(x.dtype)
        deg = jnp.sum(mask, axis=1, keepdims=True)
        agg = mask @ x / jnp.maximum(deg, 1.0)
        self_f = x @ W_self + b_self
        nb_f = agg @ W_nb + b_nb
        combined = jnp.concatenate([self_f, nb_f], axis=-1)
        out = combined @ W_comb + b_comb
        return jax.nn.relu(out)
    x = _layernorm(x + _L0_gnn_ref(x, adj, L0_gnn_W), axis=-1)
    x = _layernorm(x + _L1_gnn_ref(x, adj, L1_gnn_W_self, L1_gnn_b_self, L1_gnn_W_nb, L1_gnn_b_nb, L1_gnn_W_comb, L1_gnn_b_comb), axis=-1)
    return x

_drawn_inputs = setup_inputs


def setup_inputs(seed=0):
    import zlib

    import numpy as np

    out = dict(_drawn_inputs(seed))
    spreads = {}
    factors = {'L1_gnn_b_self': 6.225, 'L1_gnn_b_nb': 5.271, 'L1_gnn_b_comb': 3.169}
    for name, (base, spread) in spreads.items():
        noise = np.random.default_rng([zlib.crc32(name.encode()), seed]).standard_normal(out[name].shape)
        drawn = base * np.exp(spread * noise) if base else spread * noise
        out[name] = jnp.asarray(drawn.astype(out[name].dtype))
    for name, factor in factors.items():
        out[name] = (out[name] * factor).astype(out[name].dtype)
    return out
```

```python
from contextlib import ExitStack

import concourse.bass as bass
from concourse import mybir

F32, F16, F8, I32, U8 = (mybir.dt.float32, mybir.dt.float16, mybir.dt.float8e4, mybir.dt.int32,
                          mybir.dt.uint8)
ALU = mybir.AluOpType
ACT = mybir.ActivationFunctionType
AX = mybir.AxisListType

P = 128
N, D = 4096, 256
KD = D // P
NB = N // P
GB = 4
G = NB // GB
GW = GB * P
CH = NB // GB
NPAIR = G // 2
AUG = D + 2
COS_EPS = 1e-8
LN_EPS = 1e-5
UNIT_SCALE = 4096.0
MASK_ONE = 64.0
MASK_F8 = 2.0
PROB_SCALE = 4096.0
FEAT_RANGE = 16384.0
NORM_SCALE = 2048.0
EPS_MATTERS_BELOW = 0.5


def wait(engine, semaphore, value):
    if not (isinstance(value, int) and value <= 0):
        engine.wait_ge(semaphore, value)


def wait_apart(engine, semaphore, value, passed):
    engine.wait_ge(semaphore, value)
    engine.sem_inc(passed, 1)


class Steps:

    def __init__(self, engine, semaphore, base):
        self.engine, self.semaphore, self.base, self.count = engine, semaphore, base, 0

    def step(self, instruction):
        instruction.then_inc(self.semaphore, 1)
        self.count += 1
        return self.base + self.count

    def join(self, value):
        self.engine.wait_ge(self.semaphore, value)


def gnn_program(nc, xT, x, adjT, w0T, w_selfT, b_self, w_nbT, b_nb, w_comb, b_comb, out):
    mask_spill = nc.dram_tensor("mask_spill", [G, P, CH, GB * GW], U8, kind="Internal").ap()
    x1_spill = nc.dram_tensor("x1_spill", [G, P, GB, D], F32, kind="Internal").ap()
    norm_row_dram = nc.dram_tensor("norm_row_dram", [NB, P], F32, kind="Internal").ap()

    xT_v = xT.rearrange("(k p) i -> p k i", p=P)
    x_v = x.rearrange("(g q p) d -> g p q d", q=GB, p=P)
    out_v = out.rearrange("(b p) d -> b p d", p=P)
    adjT_v = adjT.rearrange("(c s p) i -> c p s i", s=GB, p=P)
    adj_diag_v = bass.AP(adjT.tensor, 0, [[N + 1, P], [P * (N + 1), NB]])

    ctx = ExitStack()
    with ctx:
        def sb(name, shape, dt):
            return ctx.enter_context(nc.sbuf_tensor(name, shape, dt))

        def sem(name):
            return ctx.enter_context(nc.semaphore(name))

        big = sb("big", [P, NB * (AUG + D) // 2], F32)
        wh = big[:, 0:NB * D].rearrange("p (b d) -> p b d", d=D)
        big16 = big[:, :].bitcast(F16)
        x1_hi = big16[:, 0:NB * AUG].rearrange("p (b d) -> p b d", d=AUG)
        x1_lo = big16[:, NB * AUG:NB * (AUG + D)].rearrange("p (b d) -> p b d", d=D)
        unitT_hi = sb("unitT_hi", [P, KD, N], F16)
        unitT_lo = sb("unitT_lo", [P, KD, N], F16)
        feat_hi = sb("feat_hi", [P, NB, AUG], F16)
        feat_lo = sb("feat_lo", [P, NB, D], F16)
        work = sb("work", [P, 8 * GW], F32)
        xT_sb = work[:, 0:4 * GW].rearrange("p (r k i) -> p r k i", r=2, k=KD)
        unit = work[:, 4 * GW:8 * GW].bitcast(F16).rearrange("p (r h b d) -> p r h b d", r=2, h=2, b=GB)
        expo = work[:, 0:4 * GW].rearrange("p (r i) -> p r i", r=GB)
        prob = work[:, 4 * GW:8 * GW].rearrange("p (r i) -> p r i", r=GB)
        prob_hi = sb("prob_hi", [P, GB, GW], F16)
        prob_lo = sb("prob_lo", [P, GB, GW], F16)
        adj_sb = sb("adj_sb", [P, 2, GB, GW], I32)
        mask = sb("mask", [P, 4, GB * GW], U8)
        mgroup = sb("mgroup", [P, 2, NB * GW], U8)
        setup_w = mgroup[:, 0, :].bitcast(F32)
        w_selfT_sb = setup_w[:, 0:KD * D].rearrange("p (k n) -> p k n", k=KD)
        w_nbT_sb = setup_w[:, KD * D:2 * KD * D].rearrange("p (k n) -> p k n", k=KD)
        w_comb_sb = setup_w[:, 2 * KD * D:4 * KD * D].rearrange("p (k n) -> p k n", k=2 * KD)
        norm_bc = mgroup[:, 1, :].bitcast(F32)
        w0T_sb = sb("w0T_sb", [P, KD, D], F32)
        mixw = sb("mixw", [P, 2 * KD, D], F32)
        bias_col = sb("bias_col", [P, 2 * KD], F32)
        bias_wide = adj_sb[:, 0, 0, :].bitcast(F32).rearrange("p (k m) -> p k m", k=2 * KD)
        bias_comb = sb("bias_comb", [1, D], F32)
        bias_bc = sb("bias_bc", [P, D], F32)
        ident = sb("ident", [P, P], F32)
        ident16 = sb("ident16", [P, P], F16)
        ones = sb("ones", [P, P], F32)
        xres = sb("xres", [P, GB, D], F32)
        rows = sb("rows", [P, GB, D], F32)
        summed = sb("summed", [P, GB, AUG], F32)
        trT = sb("trT", [P, 2, 2 * KD, P], F32)
        damp = trT[:, :, :, :].rearrange("p r k i -> p r (k i)")
        agg = sb("agg", [P, 2, D], F32)
        nsq = sb("nsq", [P, NB], F32)
        nsq_safe = sb("nsq_safe", [P, NB], F32)
        unit_mul = sb("unit_mul", [P, NB], F32)
        rnorm = sb("rnorm", [P, NB], F32)
        norm = sb("norm", [P, NB], F32)
        norm_row = sb("norm_row", [NB, P], F32)
        adj_diag = sb("adj_diag", [P, NB], I32)
        diag_a = sb("diag_a", [P, NB], F32)
        diag_b = sb("diag_b", [P, NB], F32)
        diag_e = sb("diag_e", [P, NB], F32)
        diag_w = sb("diag_w", [P, NB], F32)
        minus_half = sb("minus_half", [P, GB], F32)
        tiny = sb("tiny", [P, GB], F32)
        unit_scale = sb("unit_scale", [P, GB], F32)
        ln_eps = sb("ln_eps", [P, 1], F32)
        extremes = sb("extremes", [P, 2], F32)
        scale_row = sb("scale_row", [1, 4], F32)
        scales = sb("scales", [P, 2], F32)
        eps_flag = sb("eps_flag", [1, 1], I32)
        rsum = sb("rsum", [P, GB], F32)
        rsum_s = sb("rsum_s", [P, GB], F32)
        stats = sb("stats", [P, GB, 6], F32)
        meanvar = sb("meanvar", [P, GB, 2], F32)
        var_eps = sb("var_eps", [P, GB], F32)
        rstd = sb("rstd", [P, GB], F32)
        deg = sb("deg", [P, 2], F32)
        rdeg = sb("rdeg", [P, 2], F32)

        ps = ctx.enter_context(nc.psum_tensor("ps", [P, 8, GW], F32))

        def wh_ps(slot, b):
            return ps[:, 2 * slot + b // 2, (b % 2) * D:(b % 2 + 1) * D]

        def unitT_ps(slot, half):
            return ps[:, 4 + 2 * half + slot, :].bitcast(F16).rearrange("p (k i) -> p k i", k=KD)

        def score_ps(slot):
            return ps[:, slot, :]

        def attn_ps(q, width):
            return ps[:, 4 + q, 0:width]

        def agg_ps(slot, width):
            return ps[:, 4 + slot, 0:width]

        def tr_ps(slot):
            return ps[:, slot, :]

        def dense_ps(slot):
            return ps[:, 2 + slot, 0:D]

        sync_passed, act_passed, dve_passed = sem("sync_passed"), sem("act_passed"), sem("dve_passed")
        pe_passed, pool_passed = sem("pe_passed"), sem("pool_passed")
        w0_loaded = sem("w0_loaded")
        xT_loaded = [sem(f"xT_loaded{i}") for i in range(2)]
        setup_loaded = sem("setup_loaded")
        diag_loaded = sem("diag_loaded")
        consts_cleared = sem("consts_cleared")
        consts_ready = sem("consts_ready")
        ones_ready = sem("ones_ready")
        wh_done = sem("wh_done")
        nsq_ready = sem("nsq_ready")
        wh_copied = sem("wh_copied")
        pool_step = sem("pool_step")
        norm_ready = sem("norm_ready")
        unit_ready = sem("unit_ready")
        unitT_done = sem("unitT_done")
        unitT_hi_ready = sem("unitT_hi_ready")
        unitT_lo_ready = sem("unitT_lo_ready")
        bias_wide_ready = sem("bias_wide_ready")
        setup_done = sem("setup_done")
        setup_copied = sem("setup_copied")
        extremes_ready = sem("extremes_ready")
        extremes_turned = sem("extremes_turned")
        norms_copied = sem("norms_copied")
        norm_row_stored = sem("norm_row_stored")
        norm_bc_loaded = sem("norm_bc_loaded")
        scale_row_ready = sem("scale_row_ready")
        scales_done = sem("scales_done")
        scales_ready = sem("scales_ready")
        flag_ready = sem("flag_ready")
        diag_arg_ready = sem("diag_arg_ready")
        diag_exp_ready = sem("diag_exp_ready")
        feat_ready = sem("feat_ready")
        adj_loaded = [sem(f"adj_loaded{i}") for i in range(2)]
        mask_ready = sem("mask_ready")
        mask_stored = [sem(f"mask_stored{i}") for i in range(4)]
        score_done = sem("score_done")
        score_damped = sem("score_damped")
        exp_ready = sem("exp_ready")
        prob_ready = sem("prob_ready")
        prob_hi_ready = sem("prob_hi_ready")
        prob_lo_ready = sem("prob_lo_ready")
        attn_done = sem("attn_done")
        attn_copied = sem("attn_copied")
        xres_loaded = sem("xres_loaded")
        moments_ready = sem("moments_ready")
        rstd_ready = sem("rstd_ready")
        x1_ready = sem("x1_ready")
        x1_stored = sem("x1_stored")
        x1_hi_step = sem("x1_hi_step")
        x1_ones_ready = sem("x1_ones_ready")
        deg_step = sem("deg_step")
        dve_step = sem("dve_step")
        damp_step = sem("damp_step")
        mgroup_loaded = [sem(f"mgroup_loaded{i}") for i in range(2)]
        xb_loaded = [sem(f"xb_loaded{i}") for i in range(GB)]
        agg_done = sem("agg_done")
        rdeg_ready = sem("rdeg_ready")
        agg_ready = sem("agg_ready")
        tr_done = sem("tr_done")
        tr_ready = sem("tr_ready")
        dense_done = sem("dense_done")
        dense_read = sem("dense_read")
        y_ready = sem("y_ready")
        y_stored = [sem(f"y_stored{i}") for i in range(GB)]

        block = ctx.enter_context(nc.Block())
        PHASE1_POOL = G * 3

        @block.sync
        def _(sync):
            def load_xT(g, slot):
                sync.dma_start(xT_sb[:, slot], xT_v[:, :, bass.ds(g * GW, GW)]).then_inc(xT_loaded[slot], 16)

            sync.dma_start(w0T_sb[:, :, :], w0T.rearrange("(k p) n -> p k n", p=P)).then_inc(w0_loaded, 16)
            load_xT(0, 0)
            load_xT(1, 1)

            def load_adj(ig, c):
                sync.dma_start(adj_sb[:, c % 2], adjT_v[c, :, :, bass.ds(ig * GW, GW)]).then_inc(adj_loaded[c % 2], 16)

            for g in range(2, G):
                sync.wait_ge(wh_done, g - 1)
                load_xT(g, g % 2)
                if g == 3:
                    load_adj(0, 1)
            sync.wait_ge(setup_done, 1)
            load_adj(0, 0)
            sync.wait_ge(norms_copied, 1)
            sync.dma_start(norm_row_dram[:, :], norm_row[:, :]).then_inc(norm_row_stored, 16)
            sync.wait_ge(norm_row_stored, 16)
            sync.dma_start(norm_bc, norm_row_dram.rearrange("b p -> (b p)").partition_broadcast(P)).then_inc(norm_bc_loaded, 16)

            def group(ig, first, last):
                for c in range(CH):
                    wait_apart(sync, mask_ready, ig * CH + c + 1, sync_passed)
                    sync.dma_start(mask_spill[ig, :, c, :], mask[:, c % 4]).then_inc(mask_stored[c % 4], 16)
                    if c + 2 < CH:
                        load_adj(ig, c + 2)
                    elif not last:
                        load_adj(ig + 1, c + 2 - CH)
                    if c == 6:
                        if not first:
                            wait_apart(sync, x1_ready, ig * GB, sync_passed)
                            sync.dma_start(x1_spill[ig - 1], rows[:, :, :]).then_inc(x1_stored, 16)
                        sync.dma_start(xres[:, :, :], x_v[ig]).then_inc(xres_loaded, 16)

            group(0, True, False)
            with sync.Fori(1, G - 1) as ig:
                group(ig, False, False)
            group(G - 1, False, True)

            for i in range(4):
                sync.wait_ge(mask_stored[i], 16 * (G * CH // 4))

            def load_mgroup(ig, slot):
                sync.dma_start(mgroup[:, slot, :], mask_spill[ig].rearrange("p c i -> p (c i)")).then_inc(mgroup_loaded[slot], 16)

            load_mgroup(0, 0)
            sync.wait_ge(norm_bc_loaded, 16)
            sync.wait_ge(prob_ready, NB * G)
            load_mgroup(1, 1)
            sync.wait_ge(x1_ready, NB)
            sync.dma_start(x1_spill[G - 1], rows[:, :, :]).then_inc(x1_stored, 16)
            sync.wait_ge(x1_stored, 16 * G)

            def load_xb(ig, q):
                sync.dma_start(xres[:, q, :], x1_spill[ig, :, q, :]).then_inc(xb_loaded[q], 16)

            for q in range(GB):
                load_xb(0, q)

            def finish(ig, slot, last_pair):
                for q in range(GB):
                    wait_apart(sync, y_ready, ig * GB + q + 1, sync_passed)
                    sync.dma_start(out_v[ig * GB + q], rows[:, q, :]).then_inc(y_stored[q], 16)
                    if not (last_pair and slot == 1):
                        load_xb(ig + 1, q)
                if not last_pair:
                    load_mgroup(ig + 2, slot)

            with sync.Fori(0, NPAIR - 1) as pair:
                finish(pair * 2, 0, False)
                finish(pair * 2 + 1, 1, False)
            finish(G - 2, 0, True)
            finish(G - 1, 1, True)
            for q in range(GB):
                sync.wait_ge(y_stored[q], 16 * G)

        @block.gpsimd
        def _(pool):
            pool.memset(ident[:, :], 0.0).then_inc(consts_cleared, 1)
            pool.memset(ident16[:, :], 0.0).then_inc(consts_cleared, 1)
            pool.memset(ones[:, :], 1.0).then_inc(ones_ready, 1)
            pool.memset(tiny[:, :], 1e-36)
            pool.memset(unit_scale[:, :], UNIT_SCALE)
            pool.memset(ln_eps[:, :], LN_EPS)
            pool.memset(minus_half[:, :], -0.5).then_inc(ones_ready, 1)
            pool.wait_ge(consts_cleared, 2)
            for m in (ident, ident16):
                pool.affine_select(out=m[:, :], in_=m[:, :], compare_op=ALU.not_equal, fill=1.0, base=0,
                                   pattern=[[-1, P]], channel_multiplier=1).then_inc(consts_ready, 1)
            pool.wait_ge(ones_ready, 2)

            pool.dma_start(w_selfT_sb, w_selfT.rearrange("(k p) n -> p k n", p=P)).then_inc(setup_loaded, 16)
            pool.dma_start(w_nbT_sb, w_nbT.rearrange("(k p) n -> p k n", p=P)).then_inc(setup_loaded, 16)
            pool.dma_start(w_comb_sb, w_comb.rearrange("(k p) n -> p k n", p=P)).then_inc(setup_loaded, 16)
            with nc.allow_non_contiguous_dma(reason="biases as columns, the diagonal: single elements"):
                pool.dma_start(bias_col[:, 0:KD], b_self.rearrange("(k p) -> p k", p=P)).then_inc(setup_loaded, 16)
                pool.dma_start(bias_col[:, KD:2 * KD], b_nb.rearrange("(k p) -> p k", p=P)).then_inc(setup_loaded, 16)
                pool.dma_start(bias_comb[:, :], b_comb.rearrange("(a n) -> a n", a=1)).then_inc(setup_loaded, 16)
                pool.dma_start(adj_diag[:, :], adj_diag_v).then_inc(diag_loaded, 16)

            def norms(g):
                cols = bass.ds(g * GB, GB)
                wait_apart(pool, nsq_ready, g + 1, pool_passed)
                pool.tensor_tensor(nsq_safe[:, cols], nsq[:, cols], tiny[:, :], ALU.add).then_inc(pool_step, 1)
                wait_apart(pool, pool_step, g * 3 + 1, pool_passed)
                pool.tensor_tensor(rnorm[:, cols], nsq_safe[:, cols], minus_half[:, :], ALU.pow).then_inc(pool_step, 1)
                wait_apart(pool, pool_step, g * 3 + 2, pool_passed)
                pool.tensor_tensor(norm[:, cols], nsq[:, cols], rnorm[:, cols], ALU.mult).then_inc(pool_step, 1)
                wait_apart(pool, pool_step, g * 3 + 3, pool_passed)
                pool.tensor_tensor(unit_mul[:, cols], rnorm[:, cols], unit_scale[:, :], ALU.mult).then_inc(norm_ready, 1)

            with pool.Fori(0, G) as g:
                norms(g)

            def inv_std(b, q):
                pool.wait_ge(moments_ready, b + 1)
                pool.tensor_tensor(var_eps[:, q:q + 1], meanvar[:, q, 1:2], ln_eps[:, :], ALU.add).then_inc(pool_step, 1)
                pool.wait_ge(pool_step, PHASE1_POOL + 1 + b)
                pool.tensor_tensor(rstd[:, q:q + 1], var_eps[:, q:q + 1], minus_half[:, 0:1], ALU.pow).then_inc(rstd_ready, 1)

            with pool.Fori(0, 2 * G) as ig:
                for q in range(GB):
                    inv_std(ig * GB + q, q)

        @block.scalar
        def _(act):
            def squares(g):
                act.wait_ge(wh_copied, g + 1)
                wait(act, nsq_ready, g)
                for b in range(GB):
                    ins = act.activation(rows[:, b, :], wh[:, g * GB + b, :], ACT.Square, accum_out=nsq[:, bass.ds(g * GB + b, 1)])
                ins.then_inc(nsq_ready, 1)

            def unitT_out(g, slot):
                act.wait_ge(unitT_done, g + 1)
                act.activation(unitT_hi[:, :, bass.ds(g * GW, GW)], unitT_ps(slot, 0), ACT.Copy).then_inc(unitT_hi_ready, 1)

            squares(0)
            squares(1)
            unitT_out(0, 0)
            with act.Fori(1, NPAIR) as pair:
                squares(pair * 2)
                unitT_out(pair * 2 - 1, 1)
                squares(pair * 2 + 1)
                unitT_out(pair * 2, 0)
            unitT_out(G - 1, 1)

            act.wait_ge(setup_done, 1)
            act.activation(mixw[:, 0:KD, :], ps[:, 0, :].rearrange("p (k n) -> p k n", k=KD), ACT.Copy).then_inc(setup_copied, 1)
            act.activation(mixw[:, KD:2 * KD, :], ps[:, 1, :].rearrange("p (k n) -> p k n", k=KD), ACT.Copy).then_inc(setup_copied, 1)
            act.activation(bias_bc[:, :], ps[:, 2, 0:D], ACT.Copy).then_inc(setup_copied, 1)
            act.wait_ge(diag_arg_ready, 1)
            act.activation(diag_e[:, :], diag_a[:, :], ACT.Exp).then_inc(diag_exp_ready, 1)

            act.wait_ge(flag_ready, 1)
            eps_matters = act.value_load(eps_flag[0:1, 0:1], min_val=0, max_val=1)

            def exponentials(t, s):
                wait_apart(act, score_done, t + 1, act_passed)
                with act.If(eps_matters == 1):
                    wait_apart(act, score_damped, t + 1, act_passed)
                wait(act, prob_ready, t - GB + 1)
                act.activation(expo[:, s, :], score_ps(s), ACT.Exp, scale=1.0 / (UNIT_SCALE * UNIT_SCALE)).then_inc(exp_ready, 1)

            def heads(t, s):
                act.wait_ge(prob_ready, t + 1)
                wait(act, attn_done, t - GB + 1)
                act.activation(prob_hi[:, s, :], prob[:, s, :], ACT.Copy).then_inc(prob_hi_ready, 1)

            def chunk(g):
                t0 = g * GB
                exponentials(t0, 0)
                for s in range(1, GB):
                    exponentials(t0 + s, s)
                    heads(t0 + s - 1, s - 1)
                heads(t0 + GB - 1, GB - 1)

            chunk(0)
            with act.Fori(1, G * CH) as g:
                chunk(g)

            def mean_and_transposes(b, slot):
                act.wait_ge(agg_done, b + 1)
                act.wait_ge(rdeg_ready, b + 1)
                wait(act, tr_done, b - 1)
                act.activation(agg[:, slot, :], agg_ps(slot, D), ACT.Copy, scale=rdeg[:, slot:slot + 1]).then_inc(agg_ready, 1)
                act.wait_ge(tr_done, b + 1)
                wait(act, dense_done, b - 1)
                act.activation(trT[:, slot].rearrange("p k i -> p (k i)"), tr_ps(slot), ACT.Copy).then_inc(tr_ready, 1)

            mean_and_transposes(0, 0)
            mean_and_transposes(1, 1)
            with act.Fori(1, NB // 2) as h:
                mean_and_transposes(h * 2, 0)
                mean_and_transposes(h * 2 + 1, 1)

        @block.vector
        def _(dve):
            dve.wait_ge(setup_loaded, 16 * 6)
            dve.wait_ge(ones_ready, 2)
            for k in range(2 * KD):
                ins = dve.tensor_scalar(bias_wide[:, k, :], ones[:, :], bias_col[:, k:k + 1], None, ALU.mult)
            ins.then_inc(bias_wide_ready, 1)

            def split_units(g, slot):
                dve.wait_ge(wh_done, g + 1)
                dve.tensor_copy(wh[:, bass.ds(g * GB, GB), :].rearrange("p (a b) d -> p a (b d)", a=2),
                                ps[:, 2 * slot:2 * slot + 2, :]).then_inc(wh_copied, 1)
                dve.wait_ge(norm_ready, g + 1)
                dve.wait_ge(wh_copied, g + 1)
                wait(dve, unitT_done, g - 1)
                for b in range(GB):
                    ins = dve.tensor_scalar(unit[:, slot, 0, b, :], wh[:, g * GB + b, :],
                                            unit_mul[:, bass.ds(g * GB + b, 1)], None, ALU.mult)
                ins.then_inc(dve_step, 1)
                dve.wait_ge(dve_step, g + 1)
                for b in range(GB):
                    ins = dve.scalar_tensor_tensor(out=unit[:, slot, 1, b, :], in0=wh[:, g * GB + b, :],
                                                   scalar=unit_mul[:, bass.ds(g * GB + b, 1)],
                                                   in1=unit[:, slot, 0, b, :], op0=ALU.mult, op1=ALU.subtract)
                ins.then_inc(unit_ready, 1)

            def unitT_out(g, slot):
                dve.wait_ge(unitT_done, g + 1)
                dve.tensor_copy(unitT_lo[:, :, bass.ds(g * GW, GW)], unitT_ps(slot, 1)).then_inc(unitT_lo_ready, 1)

            split_units(0, 0)
            split_units(1, 1)
            unitT_out(0, 0)
            with dve.Fori(1, NPAIR) as pair:
                split_units(pair * 2, 0)
                unitT_out(pair * 2 - 1, 1)
                split_units(pair * 2 + 1, 1)
                unitT_out(pair * 2, 0)
            unitT_out(G - 1, 1)

            chain = Steps(dve, dve_step, G)
            dve.reduce_max(extremes[:, 0:1], norm[:, :], AX.X)
            dve.tensor_reduce(extremes[:, 1:2], norm[:, :], AX.X, ALU.min).then_inc(extremes_ready, 1)
            chain.join(chain.step(dve.tensor_scalar(diag_b[:, :], nsq[:, :], COS_EPS, None, ALU.add)))
            chain.join(chain.step(dve.reciprocal(diag_w[:, :], diag_b[:, :])))
            dve.tensor_tensor(diag_a[:, :], nsq[:, :], diag_w[:, :], ALU.mult).then_inc(diag_arg_ready, 1)
            dve.wait_ge(extremes_turned, 1)
            dve.tensor_copy(norm_row[:, :], ps[0:NB, 3, 2 * P:3 * P]).then_inc(norms_copied, 1)
            dve.reduce_max(scale_row[0:1, 2:3], ps[0:1, 3, 0:P], AX.X)
            chain.join(chain.step(dve.tensor_reduce(scale_row[0:1, 3:4], ps[0:1, 3, P:2 * P], AX.X, ALU.min)))
            dve.tensor_scalar(eps_flag[0:1, :], scale_row[0:1, 3:4], EPS_MATTERS_BELOW, None, ALU.is_lt).then_inc(flag_ready, 1)
            chain.join(chain.step(dve.tensor_scalar(scale_row[0:1, 1:2], scale_row[0:1, 2:3], 1e-30, 1.0 / FEAT_RANGE, ALU.max, ALU.mult)))
            dve.reciprocal(scale_row[0:1, 0:1], scale_row[0:1, 1:2]).then_inc(scale_row_ready, 1)
            dve.wait_ge(scales_done, 1)
            dve.tensor_copy(scales[:, :], ps[:, 3, 3 * P:3 * P + 2]).then_inc(scales_ready, 1)
            dve.wait_ge(diag_loaded, 16)
            chain.join(chain.step(dve.tensor_scalar(diag_b[:, :], adj_diag[:, :], 0.0, -PROB_SCALE, ALU.is_gt, ALU.mult)))
            dve.wait_ge(diag_exp_ready, 1)
            chain.join(chain.step(dve.scalar_tensor_tensor(out=diag_w[:, :], in0=diag_b[:, :], scalar=PROB_SCALE,
                                                           in1=diag_e[:, :], op0=ALU.add, op1=ALU.mult)))
            dve.memset(feat_hi[:, :, D:D + 1], 1.0)
            dve.wait_ge(scales_ready, 1)

            def split_features(c):
                rows_c = slice(c * GB, (c + 1) * GB)
                chain.join(chain.step(dve.tensor_scalar(feat_hi[:, rows_c, 0:D], wh[:, rows_c, :], scales[:, 0:1], None, ALU.mult)))
                dve.scalar_tensor_tensor(out=feat_lo[:, rows_c, :], in0=wh[:, rows_c, :], scalar=scales[:, 0:1],
                                         in1=feat_hi[:, rows_c, 0:D], op0=ALU.mult, op1=ALU.subtract).then_inc(feat_ready, 1)

            split_features(0)

            dve.wait_ge(flag_ready, 1)
            eps_matters = dve.value_load(eps_flag[0:1, 0:1], min_val=0, max_val=1)

            def make_mask(ig, c, slot_used):
                dve.wait_ge(adj_loaded[c % 2], (ig * (CH // 2) + c // 2 + 1) * 16)
                if slot_used:
                    dve.wait_ge(mask_stored[c % 4], (ig * (CH // 4) + c // 4) * 16)
                dve.tensor_scalar(mask[:, c % 4, :], adj_sb[:, c % 2].rearrange("p s i -> p (s i)"), 0.0, MASK_ONE,
                                  ALU.is_gt, ALU.mult).then_inc(mask_ready, 1)

            def damping(ig, jb, t, s):
                with dve.If(eps_matters == 1):
                    dve.wait_ge(norm_bc_loaded, 16)
                    dve.wait_ge(score_done, t + 1)
                    n_i = norm_bc[:, bass.ds(ig * GW, GW)]
                    n_j = norm[:, bass.ds(jb, 1)]
                    dve.tensor_scalar(damp[:, 0, :], n_i, n_j, COS_EPS, ALU.mult, ALU.add).then_inc(damp_step, 1)
                    dve.wait_ge(damp_step, t * 3 + 1)
                    dve.reciprocal(damp[:, 1, :], damp[:, 0, :]).then_inc(damp_step, 1)
                    dve.wait_ge(damp_step, t * 3 + 2)
                    dve.scalar_tensor_tensor(out=damp[:, 0, :], in0=n_i, scalar=n_j, in1=damp[:, 1, :],
                                             op0=ALU.mult, op1=ALU.mult).then_inc(damp_step, 1)
                    dve.wait_ge(damp_step, t * 3 + 3)
                    dve.tensor_tensor(score_ps(s), score_ps(s), damp[:, 0, :], ALU.mult).then_inc(score_damped, 1)

            def apply_mask(t, s, c):
                dve.wait_ge(exp_ready, t + 1)
                wait(dve, prob_hi_ready, t - GB + 1)
                dve.scalar_tensor_tensor(out=prob[:, s, :], in0=expo[:, s, :], scalar=PROB_SCALE / MASK_ONE,
                                         in1=mask[:, c % 4, s * GW:(s + 1) * GW], op0=ALU.mult, op1=ALU.mult).then_inc(prob_ready, 1)

            def tails(t, s):
                dve.wait_ge(prob_hi_ready, t + 1)
                dve.wait_ge(prob_ready, t + 1)
                dve.tensor_tensor(prob_lo[:, s, :], prob[:, s, :], prob_hi[:, s, :], ALU.subtract).then_inc(prob_lo_ready, 1)

            def attention_out(pg, q):
                dve.wait_ge(attn_done, (pg + 1) * NB)
                dve.scalar_tensor_tensor(out=summed[:, q, 0:D + 1], in0=feat_hi[:, pg * GB + q, 0:D + 1],
                                         scalar=diag_w[:, bass.ds(pg * GB + q, 1)], in1=attn_ps(q, D + 1),
                                         op0=ALU.mult, op1=ALU.add).then_inc(attn_copied, 1)

            LN_STEPS = 2 + GB * 4

            def softmax_scale(steps, pg):
                dve.wait_ge(attn_copied, (pg + 1) * GB)
                steps.join(steps.step(dve.reciprocal(rsum[:, :], summed[:, :, D])))
                steps.join(steps.step(dve.tensor_scalar(rsum_s[:, :], rsum[:, :], scales[:, 1:2], None, ALU.mult)))

            def residual_moments(steps, pg, q):
                steps.join(steps.step(dve.scalar_tensor_tensor(
                    out=summed[:, q, 0:D], in0=feat_lo[:, pg * GB + q, :], scalar=diag_w[:, bass.ds(pg * GB + q, 1)],
                    in1=summed[:, q, 0:D], op0=ALU.mult, op1=ALU.add)))
                if q == 0:
                    dve.wait_ge(xres_loaded, (pg + 1) * 16)
                steps.join(steps.step(dve.scalar_tensor_tensor(
                    out=summed[:, q, 0:D], in0=summed[:, q, 0:D], scalar=rsum_s[:, q:q + 1],
                    in1=xres[:, q, :], op0=ALU.mult, op1=ALU.add)))
                wait_apart(dve, dve_step, steps.step(dve.bn_stats(stats[:, q, :], summed[:, q, 0:D])), dve_passed)
                dve.bn_aggr(meanvar[:, q, :], stats[:, q, :]).then_inc(moments_ready, 1)

            def normalised(steps, pg, q):
                dve.wait_ge(rstd_ready, pg * GB + q + 1)
                if q == 0:
                    wait(dve, x1_stored, pg * 16)
                ready = steps.step(dve.tensor_scalar(rows[:, q, :], summed[:, q, 0:D], meanvar[:, q, 0:1],
                                                     rstd[:, q:q + 1], ALU.subtract, ALU.mult))
                steps.join(ready)
                dve.tensor_scalar(x1_hi[:, pg * GB + q, 0:D], rows[:, q, :], NORM_SCALE, None, ALU.mult).then_inc(x1_hi_step, 1)
                dve.wait_ge(x1_hi_step, pg * GB + q + 1)
                dve.scalar_tensor_tensor(out=x1_lo[:, pg * GB + q, :], in0=rows[:, q, :], scalar=NORM_SCALE,
                                         in1=x1_hi[:, pg * GB + q, 0:D], op0=ALU.mult, op1=ALU.subtract).then_inc(x1_ready, 1)

            def group(ig, first, last, steps):
                for c in range(CH):
                    t0 = ig * NB + c * GB
                    if first and c + 1 < CH:
                        split_features(c + 1)
                    if c + 1 < CH:
                        make_mask(ig, c + 1, not (first and c + 1 < 4))
                    elif not last:
                        make_mask(ig + 1, 0, True)
                    for s in range(GB):
                        damping(ig, c * GB + s, t0 + s, s)
                        apply_mask(t0 + s, s, c)
                        if s:
                            tails(t0 + s - 1, s - 1)
                    tails(t0 + GB - 1, GB - 1)
                    if not first:
                        if c == 0:
                            for q in range(GB):
                                attention_out(ig - 1, q)
                        if c == 1:
                            softmax_scale(steps, ig - 1)
                        if 1 <= c <= GB:
                            residual_moments(steps, ig - 1, c - 1)
                        if 2 <= c <= GB + 1:
                            normalised(steps, ig - 1, c - 2)

            make_mask(0, 0, False)
            group(0, True, False, None)
            dve.memset(x1_hi[:, :, D:D + 1], 1.0).then_inc(x1_ones_ready, 1)
            after_first = chain.base + chain.count
            with dve.Fori(1, G - 1) as ig:
                steps = Steps(dve, dve_step, (ig - 1) * LN_STEPS + after_first)
                group(ig, False, False, steps)
                assert steps.count == LN_STEPS
            steps = Steps(dve, dve_step, (G - 2) * LN_STEPS + after_first)
            group(G - 1, False, True, steps)
            steps = Steps(dve, dve_step, (G - 1) * LN_STEPS + after_first)
            for q in range(GB):
                attention_out(G - 1, q)
            softmax_scale(steps, G - 1)
            for q in range(GB):
                residual_moments(steps, G - 1, q)
                if q:
                    normalised(steps, G - 1, q - 1)
            normalised(steps, G - 1, GB - 1)
            after_layer0 = G * LN_STEPS + after_first

            def invert_degree(b, slot):
                dve.wait_ge(agg_done, b + 1)
                wait(dve, agg_ready, b - 1)
                dve.tensor_scalar(deg[:, slot:slot + 1], agg_ps(slot, D + 1)[:, D:D + 1], MASK_F8, NORM_SCALE,
                                  ALU.max, ALU.mult).then_inc(deg_step, 1)
                dve.wait_ge(deg_step, b + 1)
                dve.reciprocal(rdeg[:, slot:slot + 1], deg[:, slot:slot + 1]).then_inc(rdeg_ready, 1)

            def dense_out(b, ig, q):
                steps = Steps(dve, dve_step, b * 2 + after_layer0)
                dve.wait_ge(dense_done, b + 1)
                dve.tensor_tensor(summed[:, q, 0:D], dense_ps(q % 2), bias_bc[:, :], ALU.add).then_inc(dense_read, 1)
                dve.wait_ge(dense_read, b + 1)
                dve.wait_ge(xb_loaded[q], (ig + 1) * 16)
                steps.join(steps.step(dve.scalar_tensor_tensor(
                    out=summed[:, q, 0:D], in0=summed[:, q, 0:D], scalar=0.0, in1=xres[:, q, :], op0=ALU.max, op1=ALU.add)))
                wait_apart(dve, dve_step, steps.step(dve.bn_stats(stats[:, q, :], summed[:, q, 0:D])), dve_passed)
                dve.bn_aggr(meanvar[:, q, :], stats[:, q, :]).then_inc(moments_ready, 1)

            def finish(b, ig, q):
                dve.wait_ge(rstd_ready, NB + b + 1)
                wait(dve, y_stored[q], ig * 16)
                dve.tensor_scalar(rows[:, q, :], summed[:, q, 0:D], meanvar[:, q, 0:1], rstd[:, q:q + 1],
                                  ALU.subtract, ALU.mult).then_inc(y_ready, 1)

            dve.wait_ge(setup_copied, 3)
            dve.wait_ge(x1_stored, 16 * G)

            def layer1_group(ig, first):
                for q in range(GB):
                    b = ig * GB + q
                    invert_degree(b, q % 2)
                    if q:
                        finish(b - 1, ig, q - 1)
                    elif not first:
                        finish(b - 1, ig - 1, GB - 1)
                    dense_out(b, ig, q)

            layer1_group(0, True)
            with dve.Fori(1, G) as ig:
                layer1_group(ig, False)
            finish(NB - 1, G - 1, GB - 1)

        @block.tensor
        def _(pe):
            def project_group(pair, slot, first):
                g = pair * 2 + slot
                pe.wait_ge(xT_loaded[slot], pair * 16 + 16)
                if not first:
                    pe.wait_ge(wh_copied, g - 1)
                for b in range(GB):
                    for k in range(KD):
                        ins = pe.matmul(wh_ps(slot, b), xT_sb[:, slot, k, b * P:(b + 1) * P], w0T_sb[:, k, :],
                                        start=(k == 0), stop=(k == KD - 1))
                ins.then_inc(wh_done, 1)

            def turn_units(g, slot):
                pe.wait_ge(unit_ready, g + 1)
                wait(pe, unitT_hi_ready, g - 1)
                wait(pe, unitT_lo_ready, g - 1)
                for half in range(2):
                    for b in range(GB):
                        for k in range(KD):
                            ins = pe.transpose(unitT_ps(slot, half)[:, k, b * P:(b + 1) * P],
                                               unit[:, slot, half, b, k * P:(k + 1) * P], ident16[:, :])
                ins.then_inc(unitT_done, 1)

            pe.wait_ge(w0_loaded, 16)
            pe.wait_ge(consts_ready, 2)
            project_group(0, 0, True)
            project_group(0, 1, True)
            turn_units(0, 0)
            with pe.Fori(1, NPAIR) as pair:
                project_group(pair, 0, False)
                turn_units(pair * 2 - 1, 1)
                project_group(pair, 1, False)
                turn_units(pair * 2, 0)
            turn_units(G - 1, 1)

            pe.wait_ge(setup_loaded, 16 * 6)
            pe.wait_ge(bias_wide_ready, 1)
            pe.wait_ge(wh_copied, G)
            for part, w in ((0, w_selfT_sb), (1, w_nbT_sb)):
                for h in range(KD):
                    for k in range(KD):
                        pe.matmul(ps[:, part, h * D:(h + 1) * D], w[:, k, h * P:(h + 1) * P],
                                  w_comb_sb[:, part * KD + k, :], start=(k == 0), stop=(k == KD - 1))
            for k in range(2 * KD):
                pe.matmul(ps[:, 2, 0:D], bias_wide[:, k, :], w_comb_sb[:, k, :], start=(k == 0), stop=False)
            pe.matmul(ps[:, 2, 0:D], ones[0:1, :], bias_comb[0:1, :], start=False, stop=True).then_inc(setup_done, 1)

            pe.wait_ge(extremes_ready, 1)
            pe.transpose(ps[0:1, 3, 0:P], extremes[:, 0:1], ident[:, :])
            pe.transpose(ps[0:1, 3, P:2 * P], extremes[:, 1:2], ident[:, :])
            pe.transpose(ps[0:NB, 3, 2 * P:3 * P], norm[:, :], ident[:, :]).then_inc(extremes_turned, 1)
            pe.wait_ge(scale_row_ready, 1)
            pe.matmul(ps[:, 3, 3 * P:3 * P + 2], ones[0:1, :], scale_row[0:1, 0:2], start=True, stop=True).then_inc(scales_done, 1)
            pe.wait_ge(scales_ready, 1)
            pe.wait_ge(setup_copied, 3)
            pe.wait_ge(norms_copied, 1)
            pe.wait_ge(unitT_hi_ready, G)
            pe.wait_ge(unitT_lo_ready, G)

            def scores(ig, jb, t, s):
                wait(pe, exp_ready, t - GB + 1)
                src = bass.ds(jb * P, P)
                tgt = bass.ds(ig * GW, GW)
                for k in range(KD):
                    pe.matmul(score_ps(s), unitT_hi[:, k, src], unitT_lo[:, k, tgt], start=(k == 0), stop=False)
                    pe.matmul(score_ps(s), unitT_hi[:, k, src], unitT_hi[:, k, tgt], start=False, stop=False)
                    ins = pe.matmul(score_ps(s), unitT_lo[:, k, src], unitT_hi[:, k, tgt], start=False, stop=(k == KD - 1))
                ins.then_inc(score_done, 1)

            def attend(jb, t, s, start, stop, pg):
                pe.wait_ge(prob_lo_ready, t + 1)
                for q in range(GB):
                    if start and not (isinstance(pg, int) and pg == 0):
                        pe.wait_ge(attn_copied, (pg - 1) * GB + q + 1)
                    cols = slice(q * P, (q + 1) * P)
                    pe.matmul(attn_ps(q, D + 1), prob_hi[:, s, cols], feat_hi[:, jb, 0:D + 1], start=start, stop=False)
                    pe.matmul(attn_ps(q, D), prob_hi[:, s, cols], feat_lo[:, jb, :], start=False, stop=False)
                    ins = pe.matmul(attn_ps(q, D + 1), prob_lo[:, s, cols], feat_hi[:, jb, 0:D + 1], start=False, stop=stop)
                ins.then_inc(attn_done, 1)

            def chunk(ig, c, next_ig, next_c, start=False, stop=False):
                if isinstance(ig, int) and ig == 0:
                    pe.wait_ge(feat_ready, c + 1)
                t0 = ig * NB + c * GB
                for s in range(GB):
                    if next_ig is not None:
                        scores(next_ig, next_c * GB + s, t0 + GB + s, s)
                    attend(c * GB + s, t0 + s, s, start and s == 0, stop and s == GB - 1, ig)

            def group(ig, last):
                chunk(ig, 0, ig, 1, start=True)
                with pe.Fori(1, CH - 1) as c:
                    chunk(ig, c, ig, c + 1)
                chunk(ig, CH - 1, None if last else ig + 1, 0, stop=True)

            for s in range(GB):
                scores(0, s, s, s)
            group(0, False)
            with pe.Fori(1, G - 1) as ig:
                group(ig, False)
            group(G - 1, True)

            pe.wait_ge(exp_ready, G * NB)
            pe.wait_ge(x1_ones_ready, 1)

            def aggregate(pair, b, ig, q, slot, first, tail):
                if q == 0:
                    pe.wait_ge(mgroup_loaded[slot], pair * 16 + 16)
                if first:
                    if b == 0:
                        pe.wait_ge(attn_copied, NB)
                if not (isinstance(b, int) and b < 2):
                    wait_apart(pe, agg_ready, b - 1, pe_passed)
                for jb in range(NB):
                    if first and b == 0 and jb % GB == 0:
                        pe.wait_ge(x1_ready, jb + GB)
                    lhsT = mgroup[:, slot, jb * GW + q * P:jb * GW + (q + 1) * P].bitcast(F8)
                    pe.matmul(agg_ps(q % 2, D + 1), lhsT, x1_hi[:, jb, 0:D + 1], start=(jb == 0), stop=False)
                    ins = pe.matmul(agg_ps(q % 2, D), lhsT, x1_lo[:, jb, :], start=False, stop=(jb == NB - 1))
                    if jb == NB // 4 and tail is not None:
                        turn(*tail)
                    if jb == NB * 3 // 4 and tail is not None:
                        dense(*tail)
                ins.then_inc(agg_done, 1)

            def turn(b, ig, q):
                pe.wait_ge(agg_ready, b + 1)
                pe.wait_ge(xb_loaded[q], (ig + 1) * 16)
                wait(pe, tr_ready, b - 1)
                slot = q % 2
                for k in range(KD):
                    pe.transpose(tr_ps(slot)[:, k * P:(k + 1) * P], xres[:, q, k * P:(k + 1) * P], ident[:, :])
                for k in range(KD):
                    ins = pe.transpose(tr_ps(slot)[:, (KD + k) * P:(KD + k + 1) * P], agg[:, slot, k * P:(k + 1) * P], ident[:, :])
                ins.then_inc(tr_done, 1)

            def dense(b, ig, q):
                pe.wait_ge(tr_ready, b + 1)
                wait(pe, dense_read, b - 1)
                for k in range(2 * KD):
                    ins = pe.matmul(dense_ps(q % 2), trT[:, q % 2, k, :], mixw[:, k, :], start=(k == 0), stop=(k == 2 * KD - 1))
                ins.then_inc(dense_done, 1)

            def layer1_pair(pair, first):
                for half in range(2):
                    ig = pair * 2 + half
                    for q in range(GB):
                        b = ig * GB + q
                        if q:
                            tail = (b - 1, ig, q - 1)
                        elif first and half == 0:
                            tail = None
                        else:
                            tail = (b - 1, ig - 1, GB - 1)
                        aggregate(pair, b, ig, q, half, first, tail)

            layer1_pair(0, True)
            with pe.Fori(1, NPAIR) as pair:
                layer1_pair(pair, False)
            turn(NB - 1, G - 1, GB - 1)
            dense(NB - 1, G - 1, GB - 1)


def kernel(x, adj, L0_gnn_W, L1_gnn_W_self, L1_gnn_b_self, L1_gnn_W_nb, L1_gnn_b_nb, L1_gnn_W_comb, L1_gnn_b_comb):
    import numpy as np
    import concourse.bacc as bacc
    from concourse.bass_utils import run_bass_kernel_spmd

    arrays = {
        "xT": np.ascontiguousarray(np.asarray(x).T),
        "x": np.ascontiguousarray(np.asarray(x)),
        "adjT": np.ascontiguousarray(np.asarray(adj).T),
        "w0T": np.ascontiguousarray(np.asarray(L0_gnn_W).T),
        "w_selfT": np.ascontiguousarray(np.asarray(L1_gnn_W_self).T),
        "b_self": np.ascontiguousarray(np.asarray(L1_gnn_b_self)),
        "w_nbT": np.ascontiguousarray(np.asarray(L1_gnn_W_nb).T),
        "b_nb": np.ascontiguousarray(np.asarray(L1_gnn_b_nb)),
        "w_comb": np.ascontiguousarray(np.asarray(L1_gnn_W_comb)),
        "b_comb": np.ascontiguousarray(np.asarray(L1_gnn_b_comb)),
    }
    nc = bacc.Bacc("TRN2", target_bir_lowering=False, num_devices=1)
    args = [nc.dram_tensor(name, a.shape, mybir.dt.from_np(a.dtype), kind="ExternalInput").ap()
            for name, a in arrays.items()]
    out = nc.dram_tensor("out", (N, D), F32, kind="ExternalOutput").ap()
    gnn_program(nc, *args, out)
    r = run_bass_kernel_spmd(nc, [arrays], core_ids=[0])
    return r.results[0]["out"]
```

```python
from contextlib import ExitStack

import concourse.bass as bass
from concourse import mybir

F32, F16, F8, I32, U8 = (mybir.dt.float32, mybir.dt.float16, mybir.dt.float8e4, mybir.dt.int32,
                          mybir.dt.uint8)
ALU = mybir.AluOpType
ACT = mybir.ActivationFunctionType
AX = mybir.AxisListType

P = 128
N, D = 4096, 256
KD = D // P
NB = N // P
GB = 4
G = NB // GB
GW = GB * P
CH = NB // GB
NPAIR = G // 2
HW = GW // 2
STEP_TILES = 2 * GB
DIRECT = {0: 0, 1: 1, 4: 2, 5: 3}
TURNED = {2: (0, 0), 3: (0, 1), 6: (1, 0), 7: (1, 1)}
AHEAD = 3
AUG = D + 2
COS_EPS = 1e-8
LN_EPS = 1e-5
UNIT_SCALE = 4096.0
PROB_SCALE = 4096.0
FEAT_RANGE = 16384.0
NORM_SCALE = 2048.0
EPS_MATTERS_BELOW = 0.5


def wait(engine, semaphore, value):
    if not (isinstance(value, int) and value <= 0):
        engine.wait_ge(semaphore, value)


def wait_apart(engine, semaphore, value, passed):
    wait(engine, semaphore, value)
    if not isinstance(value, int):
        engine.sem_inc(passed, 1)


def tiles_before(a):
    pairs = sum(G - 1 - k for k in range(a))
    return GB * a + STEP_TILES * pairs, GB * (a + pairs), (GB * a + STEP_TILES * pairs) // 2


class Steps:

    def __init__(self, engine, semaphore, base):
        self.engine, self.semaphore, self.base, self.count = engine, semaphore, base, 0

    def step(self, instruction):
        instruction.then_inc(self.semaphore, 1)
        self.count += 1
        return self.base + self.count

    def join(self, value):
        self.engine.wait_ge(self.semaphore, value)


def gnn_program(nc, xT, x, adjT, w0T, w_selfT, b_self, w_nbT, b_nb, w_comb, b_comb, out):
    mask_spill = nc.dram_tensor("mask_spill", [G, P, NB, GW], U8, kind="Internal").ap()
    x1_spill = nc.dram_tensor("x1_spill", [G, P, GB, D], F32, kind="Internal").ap()
    norm_row_dram = nc.dram_tensor("norm_row_dram", [NB, P], F32, kind="Internal").ap()

    xT_v = xT.rearrange("(k p) i -> p k i", p=P)
    x_v = x.rearrange("(g q p) d -> g p q d", q=GB, p=P)
    out_v = out.rearrange("(b p) d -> b p d", p=P)
    adjT_v = adjT.rearrange("(c s p) i -> c p s i", s=GB, p=P)
    adj_diag_v = bass.AP(adjT.tensor, 0, [[N + 1, P], [P * (N + 1), NB]])

    ctx = ExitStack()
    with ctx:
        def sb(name, shape, dt):
            return ctx.enter_context(nc.sbuf_tensor(name, shape, dt))

        def sem(name):
            return ctx.enter_context(nc.semaphore(name))

        big = sb("big", [P, G, GB * (AUG + D) // 2], F32)
        big16 = big[:, :, :].bitcast(F16)

        def wh_of(g):
            return big[:, g, 0:GB * D].rearrange("p (b d) -> p b d", d=D)

        def partial_of(g):
            return big[:, g, 0:GB * (D + 1)].rearrange("p (b d) -> p b d", d=D + 1)

        def x1_hi_of(g):
            return big16[:, g, 0:GB * AUG].rearrange("p (b d) -> p b d", d=AUG)

        def x1_lo_of(g):
            return big16[:, g, GB * AUG:GB * (AUG + D)].rearrange("p (b d) -> p b d", d=D)

        unitT_hi = sb("unitT_hi", [P, KD, N], F16)
        unitT_lo = sb("unitT_lo", [P, KD, N], F16)
        feat_hi = sb("feat_hi", [P, NB, AUG], F16)
        feat_lo = sb("feat_lo", [P, NB, D], F16)
        work = sb("work", [P, 8 * GW], F32)
        xT_sb = feat_lo[:, :, :].bitcast(F32).rearrange("p b d -> p (b d)").rearrange("p (r k i) -> p r k i", r=4, k=KD)
        unit = work[:, 4 * GW:8 * GW].bitcast(F16).rearrange("p (r h b d) -> p r h b d", r=2, h=2, b=GB)
        expo = work[:, 0:4 * GW].rearrange("p (r i) -> p r i", r=GB)
        prob = work[:, 4 * GW:8 * GW].rearrange("p (r i) -> p r i", r=GB)
        prob_hi = sb("prob_hi", [P, GB, GW], F16)
        prob_lo = sb("prob_lo", [P, GB, GW], F16)
        adj_sb = sb("adj_sb", [P, 4, 2 * GW], I32)
        mask = sb("mask", [P, 4, 2 * GW], F8)
        mgroup = sb("mgroup", [P, 2, NB * GW], F8)
        setup_w = mgroup[:, 0, :].bitcast(F32)
        w_selfT_sb = setup_w[:, 0:KD * D].rearrange("p (k n) -> p k n", k=KD)
        w_nbT_sb = setup_w[:, KD * D:2 * KD * D].rearrange("p (k n) -> p k n", k=KD)
        w_comb_sb = setup_w[:, 2 * KD * D:4 * KD * D].rearrange("p (k n) -> p k n", k=2 * KD)
        norm_bc = mgroup[:, 1, :].bitcast(F32)
        w0T_sb = sb("w0T_sb", [P, KD, D], F32)
        mixw = sb("mixw", [P, 2 * KD, D], F32)
        bias_col = sb("bias_col", [P, 2 * KD], F32)
        agg_rows = sb("agg_rows", [P, 2 * D], F32)
        agg = agg_rows[:, :].rearrange("p (r d) -> p r d", r=2)
        bias_wide = agg_rows[:, :].rearrange("p (k m) -> p k m", k=2 * KD)
        bias_comb = sb("bias_comb", [1, D], F32)
        bias_bc = sb("bias_bc", [P, D], F32)
        ident = sb("ident", [P, P], F32)
        ident16 = sb("ident16", [P, P], F16)
        ones = sb("ones", [P, P], F32)
        xres = sb("xres", [P, GB, D], F32)
        rows = sb("rows", [P, GB, D], F32)
        summed = sb("summed", [P, GB, AUG], F32)
        trT = sb("trT", [P, 2, 2 * KD, P], F32)
        damp = trT[:, :, :, :].rearrange("p r k i -> p r (k i)")
        nsq = sb("nsq", [P, NB], F32)
        nsq_safe = sb("nsq_safe", [P, NB], F32)
        unit_mul = sb("unit_mul", [P, NB], F32)
        rnorm = sb("rnorm", [P, NB], F32)
        norm = sb("norm", [P, NB], F32)
        norm_row = sb("norm_row", [NB, P], F32)
        adj_diag = sb("adj_diag", [P, NB], I32)
        diag_a = sb("diag_a", [P, NB], F32)
        diag_b = sb("diag_b", [P, NB], F32)
        diag_e = sb("diag_e", [P, NB], F32)
        diag_w = sb("diag_w", [P, NB], F32)
        minus_half = sb("minus_half", [P, GB], F32)
        tiny = sb("tiny", [P, GB], F32)
        unit_scale = sb("unit_scale", [P, GB], F32)
        ln_eps = sb("ln_eps", [P, 1], F32)
        extremes = sb("extremes", [P, 2], F32)
        scale_row = sb("scale_row", [1, 4], F32)
        scales = sb("scales", [P, 2], F32)
        eps_flag = sb("eps_flag", [1, 1], I32)
        rsum = sb("rsum", [P, GB], F32)
        rsum_s = sb("rsum_s", [P, GB], F32)
        stats = sb("stats", [P, GB, 6], F32)
        meanvar = sb("meanvar", [P, GB, 2], F32)
        var_eps = sb("var_eps", [P, GB], F32)
        rstd = sb("rstd", [P, GB], F32)
        deg = sb("deg", [P, 2], F32)
        rdeg = sb("rdeg", [P, 2], F32)

        ps = ctx.enter_context(nc.psum_tensor("ps", [P, 8, GW], F32))

        def wh_ps(slot, b):
            return ps[:, 2 * slot + b // 2, (b % 2) * D:(b % 2 + 1) * D]

        def unitT_ps(slot, half):
            return ps[:, 4 + 2 * half + slot, :].bitcast(F16).rearrange("p (k i) -> p k i", k=KD)

        def score_ps(tile):
            return ps[:, tile % 2, :]

        def turned_ps(u, width):
            return ps[:, 2 + u, 0:width]

        def attn_ps(q, width):
            return ps[:, 4 + q, 0:width]

        def agg_ps(slot, width):
            return ps[:, 4 + slot, 0:width]

        def tr_ps(slot):
            return ps[:, slot, :]

        def dense_ps(slot):
            return ps[:, 2 + slot, 0:D]

        sync_passed, act_passed, dve_passed = sem("sync_passed"), sem("act_passed"), sem("dve_passed")
        pe_passed, pool_passed = sem("pe_passed"), sem("pool_passed")
        w0_loaded = sem("w0_loaded")
        xT_loaded = [sem(f"xT_loaded{i}") for i in range(4)]
        setup_loaded = sem("setup_loaded")
        diag_loaded = sem("diag_loaded")
        consts_cleared = sem("consts_cleared")
        consts_ready = sem("consts_ready")
        ones_ready = sem("ones_ready")
        wh_done = sem("wh_done")
        nsq_ready = sem("nsq_ready")
        wh_copied = sem("wh_copied")
        pool_step = sem("pool_step")
        norm_ready = sem("norm_ready")
        unit_ready = sem("unit_ready")
        unitT_done = sem("unitT_done")
        unitT_hi_ready = sem("unitT_hi_ready")
        unitT_lo_ready = sem("unitT_lo_ready")
        bias_wide_ready = sem("bias_wide_ready")
        setup_done = sem("setup_done")
        setup_copied = sem("setup_copied")
        extremes_ready = sem("extremes_ready")
        extremes_turned = sem("extremes_turned")
        norms_copied = sem("norms_copied")
        norm_row_stored = sem("norm_row_stored")
        norm_bc_loaded = sem("norm_bc_loaded")
        scale_row_ready = sem("scale_row_ready")
        scales_done = sem("scales_done")
        scales_ready = sem("scales_ready")
        flag_ready = sem("flag_ready")
        diag_arg_ready = sem("diag_arg_ready")
        diag_exp_ready = sem("diag_exp_ready")
        feat_ready = sem("feat_ready")
        adj_loaded = [sem(f"adj_loaded{i}") for i in range(4)]
        mask_ready = sem("mask_ready")
        mask_stored = [sem(f"mask_stored{i}") for i in range(4)]
        score_done = sem("score_done")
        score_damped = sem("score_damped")
        exp_ready = sem("exp_ready")
        prob_ready = sem("prob_ready")
        prob_hi_ready = sem("prob_hi_ready")
        prob_lo_ready = sem("prob_lo_ready")
        attn_done = sem("attn_done")
        turned_copied = sem("turned_copied")
        attn_copied = sem("attn_copied")
        xres_loaded = sem("xres_loaded")
        moments_ready = sem("moments_ready")
        rstd_ready = sem("rstd_ready")
        x1_ready = sem("x1_ready")
        x1_stored = sem("x1_stored")
        feat_hi_step = sem("feat_hi_step")
        x1_ones_ready = sem("x1_ones_ready")
        summed_ready = sem("summed_ready")
        deg_step = sem("deg_step")
        dve_step = sem("dve_step")
        damp_step = sem("damp_step")
        mgroup_loaded = [sem(f"mgroup_loaded{i}") for i in range(2)]
        xb_loaded = [sem(f"xb_loaded{i}") for i in range(GB)]
        agg_done = sem("agg_done")
        rdeg_ready = sem("rdeg_ready")
        agg_ready = sem("agg_ready")
        tr_done = sem("tr_done")
        tr_ready = sem("tr_ready")
        dense_done = sem("dense_done")
        dense_read = sem("dense_read")
        y_ready = sem("y_ready")
        y_stored = [sem(f"y_stored{i}") for i in range(GB)]

        block = ctx.enter_context(nc.Block())
        PHASE0_POOL = G * 3

        @block.sync
        def _(sync):
            def load_xT(g):
                sync.dma_start(xT_sb[:, g % 4], xT_v[:, :, g * GW:(g + 1) * GW]).then_inc(xT_loaded[g % 4], 16)

            sync.dma_start(w0T_sb[:, :, :], w0T.rearrange("(k p) n -> p k n", p=P)).then_inc(w0_loaded, 16)
            for g in range(4):
                load_xT(g)

            def load_direct(a, b, m, slot):
                sync.dma_start(adj_sb[:, slot, :].rearrange("p (s i) -> p s i", s=2),
                               adjT_v[b, :, 2 * m:2 * m + 2, a * GW:(a + 1) * GW]).then_inc(adj_loaded[slot], 16)

            def load_turned(a, b, h, slot):
                sync.dma_start(adj_sb[:, slot, :].rearrange("p (s i) -> p s i", s=GB),
                               adjT_v[a, :, :, bass.ds(b * GW + h * HW, HW)]).then_inc(adj_loaded[slot], 16)

            def load_unit(a, b, m, slot):
                if m % 2 == 0:
                    load_direct(a, b, m // 2, slot)
                else:
                    load_turned(a, b, m // 2, slot)

            def store_direct(a, b, m, slot):
                sync.dma_start(mask_spill[a, :, bass.ds(b * GB + 2 * m, 2), :],
                               mask[:, slot, :].bitcast(U8).rearrange("p (s i) -> p s i", s=2)).then_inc(mask_stored[slot], 16)

            def store_turned(a, b, h, slot):
                sync.dma_start(mask_spill[b, :, a * GB:(a + 1) * GB, h * HW:(h + 1) * HW],
                               mask[:, slot, :].bitcast(U8).rearrange("p (s i) -> p s i", s=GB)).then_inc(mask_stored[slot], 16)

            load_direct(0, 0, 0, 0)
            load_direct(0, 0, 1, 1)
            for g in range(4, G):
                sync.wait_ge(wh_done, g - 3)
                load_xT(g)
            load_unit(0, 1, 0, 2)
            load_unit(0, 1, 1, 3)
            sync.wait_ge(norms_copied, 1)
            sync.dma_start(norm_row_dram[:, :], norm_row[:, :]).then_inc(norm_row_stored, 16)
            sync.wait_ge(norm_row_stored, 16)
            sync.dma_start(norm_bc, norm_row_dram.rearrange("b p -> (b p)").partition_broadcast(P)).then_inc(norm_bc_loaded, 16)

            def diagonal(a):
                u0 = tiles_before(a)[2]
                for m in range(2):
                    sync.wait_ge(mask_ready, u0 + m + 1)
                    store_direct(a, a, m, (u0 + m) % 4)
                    if a + 1 < G:
                        load_unit(a, a + 1, m + 2, (u0 + m) % 4)

            def pair(a, b, last):
                u0 = tiles_before(a)[2] + 2
                for m in range(4):
                    slot = (u0 + m) % 4
                    wait_apart(sync, mask_ready, (b - a - 1) * 4 + (u0 + m + 1), sync_passed)
                    if m % 2 == 0:
                        store_direct(a, b, m // 2, slot)
                    else:
                        store_turned(a, b, m // 2, slot)
                    if not last:
                        load_unit(a, b + 1, m, slot)
                    elif m < 2:
                        load_direct(a + 1, a + 1, m, slot)
                    elif a + 2 < G:
                        load_unit(a + 1, a + 2, m - 2, slot)

            for a in range(G):
                diagonal(a)
                if a < G - 2:
                    with sync.Fori(a + 1, G - 1) as b:
                        pair(a, b, False)
                if a < G - 1:
                    pair(a, G - 1, True)
                if a:
                    sync.wait_ge(x1_ready, a * GB)
                    sync.dma_start(x1_spill[a - 1], rows[:, :, :]).then_inc(x1_stored, 16)
                sync.dma_start(xres[:, :, :], x_v[a]).then_inc(xres_loaded, 16)

            for i in range(4):
                sync.wait_ge(mask_stored[i], 16 * (G * CH * 2 // 4))

            def load_mgroup(ig, slot):
                sync.dma_start(mgroup[:, slot, :].bitcast(U8), mask_spill[ig].rearrange("p b i -> p (b i)")).then_inc(mgroup_loaded[slot], 16)

            load_mgroup(0, 0)
            sync.wait_ge(norm_bc_loaded, 16)
            sync.wait_ge(prob_ready, NB * G)
            load_mgroup(1, 1)
            sync.wait_ge(x1_ready, NB)
            sync.dma_start(x1_spill[G - 1], rows[:, :, :]).then_inc(x1_stored, 16)
            sync.wait_ge(x1_stored, 16 * G)

            def load_xb(ig, q):
                sync.dma_start(xres[:, q, :], x1_spill[ig, :, q, :]).then_inc(xb_loaded[q], 16)

            for q in range(GB):
                load_xb(0, q)

            def finish(ig, slot, last_pair):
                for q in range(GB):
                    wait_apart(sync, y_ready, ig * GB + q + 1, sync_passed)
                    sync.dma_start(out_v[ig * GB + q], rows[:, q, :]).then_inc(y_stored[q], 16)
                    if not (last_pair and slot == 1):
                        load_xb(ig + 1, q)
                if not last_pair:
                    load_mgroup(ig + 2, slot)

            with sync.Fori(0, NPAIR - 1) as pair:
                finish(pair * 2, 0, False)
                finish(pair * 2 + 1, 1, False)
            finish(G - 2, 0, True)
            finish(G - 1, 1, True)
            for q in range(GB):
                sync.wait_ge(y_stored[q], 16 * G)

        @block.gpsimd
        def _(pool):
            pool.memset(ident[:, :], 0.0).then_inc(consts_cleared, 1)
            pool.memset(ident16[:, :], 0.0).then_inc(consts_cleared, 1)
            pool.memset(ones[:, :], 1.0).then_inc(ones_ready, 1)
            pool.memset(tiny[:, :], 1e-36)
            pool.memset(unit_scale[:, :], UNIT_SCALE)
            pool.memset(ln_eps[:, :], LN_EPS)
            pool.memset(minus_half[:, :], -0.5).then_inc(ones_ready, 1)
            pool.wait_ge(consts_cleared, 2)
            for m in (ident, ident16):
                pool.affine_select(out=m[:, :], in_=m[:, :], compare_op=ALU.not_equal, fill=1.0, base=0,
                                   pattern=[[-1, P]], channel_multiplier=1).then_inc(consts_ready, 1)
            pool.wait_ge(ones_ready, 2)

            pool.dma_start(w_selfT_sb, w_selfT.rearrange("(k p) n -> p k n", p=P)).then_inc(setup_loaded, 16)
            pool.dma_start(w_nbT_sb, w_nbT.rearrange("(k p) n -> p k n", p=P)).then_inc(setup_loaded, 16)
            pool.dma_start(w_comb_sb, w_comb.rearrange("(k p) n -> p k n", p=P)).then_inc(setup_loaded, 16)
            with nc.allow_non_contiguous_dma(reason="biases as columns, the diagonal: single elements"):
                pool.dma_start(bias_col[:, 0:KD], b_self.rearrange("(k p) -> p k", p=P)).then_inc(setup_loaded, 16)
                pool.dma_start(bias_col[:, KD:2 * KD], b_nb.rearrange("(k p) -> p k", p=P)).then_inc(setup_loaded, 16)
                pool.dma_start(bias_comb[:, :], b_comb.rearrange("(a n) -> a n", a=1)).then_inc(setup_loaded, 16)
                pool.dma_start(adj_diag[:, :], adj_diag_v).then_inc(diag_loaded, 16)

            def norms(g):
                cols = slice(g * GB, (g + 1) * GB)
                pool.wait_ge(nsq_ready, g + 1)
                pool.tensor_tensor(nsq_safe[:, cols], nsq[:, cols], tiny[:, :], ALU.add).then_inc(pool_step, 1)
                pool.wait_ge(pool_step, g * 3 + 1)
                pool.tensor_tensor(rnorm[:, cols], nsq_safe[:, cols], minus_half[:, :], ALU.pow).then_inc(pool_step, 1)
                pool.wait_ge(pool_step, g * 3 + 2)
                pool.tensor_tensor(norm[:, cols], nsq[:, cols], rnorm[:, cols], ALU.mult).then_inc(pool_step, 1)
                pool.wait_ge(pool_step, g * 3 + 3)
                pool.tensor_tensor(unit_mul[:, cols], rnorm[:, cols], unit_scale[:, :], ALU.mult).then_inc(norm_ready, 1)

            for g in range(G):
                norms(g)

            def inv_std(b, q):
                pool.wait_ge(moments_ready, b + 1)
                pool.tensor_tensor(var_eps[:, q:q + 1], meanvar[:, q, 1:2], ln_eps[:, :], ALU.add).then_inc(pool_step, 1)
                pool.wait_ge(pool_step, PHASE0_POOL + 1 + b)
                pool.tensor_tensor(rstd[:, q:q + 1], var_eps[:, q:q + 1], minus_half[:, 0:1], ALU.pow).then_inc(rstd_ready, 1)

            with pool.Fori(0, 2 * G) as ig:
                for q in range(GB):
                    inv_std(ig * GB + q, q)

        @block.scalar
        def _(act):
            def squares(g):
                act.wait_ge(wh_copied, g + 1)
                wait(act, nsq_ready, g)
                for b in range(GB):
                    ins = act.activation(rows[:, b, :], wh_of(g)[:, b, :], ACT.Square,
                                         accum_out=nsq[:, g * GB + b:g * GB + b + 1])
                ins.then_inc(nsq_ready, 1)

            def unitT_out(g):
                act.wait_ge(unitT_done, g + 1)
                act.activation(unitT_hi[:, :, g * GW:(g + 1) * GW], unitT_ps(g % 2, 0), ACT.Copy).then_inc(unitT_hi_ready, 1)

            squares(0)
            for g in range(1, G):
                squares(g)
                unitT_out(g - 1)
            unitT_out(G - 1)

            act.wait_ge(setup_done, 1)
            act.activation(mixw[:, 0:KD, :], ps[:, 2, :].rearrange("p (k n) -> p k n", k=KD), ACT.Copy).then_inc(setup_copied, 1)
            act.activation(mixw[:, KD:2 * KD, :], ps[:, 3, :].rearrange("p (k n) -> p k n", k=KD), ACT.Copy).then_inc(setup_copied, 1)
            act.activation(bias_bc[:, :], ps[:, 4, 0:D], ACT.Copy).then_inc(setup_copied, 1)
            act.wait_ge(diag_arg_ready, 1)
            act.activation(diag_e[:, :], diag_a[:, :], ACT.Exp).then_inc(diag_exp_ready, 1)

            act.wait_ge(flag_ready, 1)
            eps_matters = act.value_load(eps_flag[0:1, 0:1], min_val=0, max_val=1)

            def exponentials(t, f, r):
                wait_apart(act, score_done, t + 1, act_passed)
                with act.If(eps_matters == 1):
                    wait_apart(act, score_damped, f + 1, act_passed)
                wait(act, prob_ready, t - GB + 1)
                act.activation(expo[:, r, :], score_ps(r), ACT.Exp, scale=1.0 / (UNIT_SCALE * UNIT_SCALE)).then_inc(exp_ready, 1)

            def heads(t, s):
                act.wait_ge(prob_ready, t + 1)
                wait(act, attn_done, t - GB + 1)
                act.activation(prob_hi[:, s, :], prob[:, s, :], ACT.Copy, scale=PROB_SCALE).then_inc(prob_hi_ready, 1)

            def unit_mask(u_slot, s, stored):
                wait_apart(act, mask_stored[u_slot], stored, act_passed)
                act.activation(mask[:, u_slot, :], prob[:, s:s + 2, :].rearrange("p r i -> p (r i)"), ACT.Sign,
                               saturate=False).then_inc(mask_ready, 1)

            def diagonal(a):
                t0, f0, u0 = tiles_before(a)
                exponentials(t0, f0, 0)
                for j in range(GB):
                    if j + 1 < GB:
                        exponentials(t0 + j + 1, f0 + j + 1, j + 1)
                    heads(t0 + j, j)
                    if j % 2:
                        u = u0 + j // 2
                        unit_mask(u % 4, j - 1, 16 * (u // 4))

            def pair(a, b):
                t0, f0, u0 = (first + more for first, more in zip(tiles_before(a), (GB, GB, 2)))
                n = b - a - 1
                tile = lambda j: n * STEP_TILES + (t0 + j)
                exponentials(tile(0), n * GB + f0, 0)
                exponentials(tile(1), n * GB + (f0 + 1), 1)
                for j in range(STEP_TILES):
                    if j in (2, 3):
                        exponentials(tile(j + 2), n * GB + (f0 + j), j)
                    heads(tile(j), j % GB)
                    if j % 2:
                        m = j // 2
                        unit_mask((u0 + m) % 4, (j - 1) % GB, n * 16 + 16 * ((u0 + m) // 4))

            for a in range(G):
                diagonal(a)
                if a == 0:
                    pair(0, 1)
                if a < G - 2:
                    with act.Fori(max(a + 1, 2), G - 1) as b:
                        pair(a, b)
                if a < G - 1:
                    pair(a, G - 1)

            def mean_and_transposes(b, slot):
                act.wait_ge(agg_done, b + 1)
                act.wait_ge(rdeg_ready, b + 1)
                wait(act, tr_done, b - 1)
                act.activation(agg[:, slot, :], agg_ps(slot, D), ACT.Copy, scale=rdeg[:, slot:slot + 1]).then_inc(agg_ready, 1)
                act.wait_ge(tr_done, b + 1)
                wait(act, dense_done, b - 1)
                act.activation(trT[:, slot].rearrange("p k i -> p (k i)"), tr_ps(slot), ACT.Copy).then_inc(tr_ready, 1)

            mean_and_transposes(0, 0)
            mean_and_transposes(1, 1)
            with act.Fori(1, NB // 2) as h:
                mean_and_transposes(h * 2, 0)
                mean_and_transposes(h * 2 + 1, 1)

        @block.vector
        def _(dve):
            dve.wait_ge(setup_loaded, 16 * 6)
            dve.wait_ge(ones_ready, 2)
            for k in range(2 * KD):
                ins = dve.tensor_scalar(bias_wide[:, k, :], ones[:, :], bias_col[:, k:k + 1], None, ALU.mult)
            ins.then_inc(bias_wide_ready, 1)

            def copy_wh(g):
                dve.wait_ge(wh_done, g + 1)
                dve.tensor_copy(wh_of(g).rearrange("p (a b) d -> p a (b d)", a=2),
                                ps[:, 2 * (g % 2):2 * (g % 2) + 2, :]).then_inc(wh_copied, 1)

            def split_units(g):
                dve.wait_ge(norm_ready, g + 1)
                dve.wait_ge(wh_copied, g + 1)
                wait(dve, unitT_done, g - 1)
                for b in range(GB):
                    ins = dve.tensor_scalar(unit[:, g % 2, 0, b, :], wh_of(g)[:, b, :],
                                            unit_mul[:, g * GB + b:g * GB + b + 1], None, ALU.mult)
                ins.then_inc(dve_step, 1)
                dve.wait_ge(dve_step, g + 1)
                for b in range(GB):
                    ins = dve.scalar_tensor_tensor(out=unit[:, g % 2, 1, b, :], in0=wh_of(g)[:, b, :],
                                                   scalar=unit_mul[:, g * GB + b:g * GB + b + 1],
                                                   in1=unit[:, g % 2, 0, b, :], op0=ALU.mult, op1=ALU.subtract)
                ins.then_inc(unit_ready, 1)

            def unitT_out(g):
                dve.wait_ge(unitT_done, g + 1)
                dve.tensor_copy(unitT_lo[:, :, g * GW:(g + 1) * GW], unitT_ps(g % 2, 1)).then_inc(unitT_lo_ready, 1)

            copy_wh(0)
            for g in range(G):
                if g + 1 < G:
                    copy_wh(g + 1)
                split_units(g)
                if g:
                    unitT_out(g - 1)
            unitT_out(G - 1)

            chain = Steps(dve, dve_step, G)
            dve.reduce_max(extremes[:, 0:1], norm[:, :], AX.X)
            dve.tensor_reduce(extremes[:, 1:2], norm[:, :], AX.X, ALU.min).then_inc(extremes_ready, 1)
            chain.join(chain.step(dve.tensor_scalar(diag_b[:, :], nsq[:, :], COS_EPS, None, ALU.add)))
            chain.join(chain.step(dve.reciprocal(diag_w[:, :], diag_b[:, :])))
            dve.tensor_tensor(diag_a[:, :], nsq[:, :], diag_w[:, :], ALU.mult).then_inc(diag_arg_ready, 1)
            dve.wait_ge(extremes_turned, 1)
            dve.tensor_copy(norm_row[:, :], ps[0:NB, 5, 2 * P:3 * P]).then_inc(norms_copied, 1)
            dve.reduce_max(scale_row[0:1, 2:3], ps[0:1, 5, 0:P], AX.X)
            chain.join(chain.step(dve.tensor_reduce(scale_row[0:1, 3:4], ps[0:1, 5, P:2 * P], AX.X, ALU.min)))
            dve.tensor_scalar(eps_flag[0:1, :], scale_row[0:1, 3:4], EPS_MATTERS_BELOW, None, ALU.is_lt).then_inc(flag_ready, 1)
            chain.join(chain.step(dve.tensor_scalar(scale_row[0:1, 1:2], scale_row[0:1, 2:3], 1e-30, 1.0 / FEAT_RANGE, ALU.max, ALU.mult)))
            dve.reciprocal(scale_row[0:1, 0:1], scale_row[0:1, 1:2]).then_inc(scale_row_ready, 1)
            dve.wait_ge(scales_done, 1)
            dve.tensor_copy(scales[:, :], ps[:, 5, 3 * P:3 * P + 2]).then_inc(scales_ready, 1)
            dve.wait_ge(diag_loaded, 16)
            chain.join(chain.step(dve.tensor_scalar(diag_b[:, :], adj_diag[:, :], 0.0, -PROB_SCALE, ALU.is_gt, ALU.mult)))
            dve.wait_ge(diag_exp_ready, 1)
            chain.join(chain.step(dve.scalar_tensor_tensor(out=diag_w[:, :], in0=diag_b[:, :], scalar=PROB_SCALE,
                                                           in1=diag_e[:, :], op0=ALU.add, op1=ALU.mult)))
            dve.memset(feat_hi[:, :, D:D + 1], 1.0)
            dve.wait_ge(scales_ready, 1)

            def split_features(g):
                grp = bass.ds(g * GB, GB)
                dve.tensor_scalar(feat_hi[:, grp, 0:D], wh_of(g), scales[:, 0:1], None, ALU.mult).then_inc(feat_hi_step, 1)
                dve.wait_ge(feat_hi_step, g + 1)
                dve.scalar_tensor_tensor(out=feat_lo[:, grp, :], in0=wh_of(g), scalar=scales[:, 0:1],
                                         in1=feat_hi[:, grp, 0:D], op0=ALU.mult, op1=ALU.subtract).then_inc(feat_ready, 1)

            split_features(0)

            dve.wait_ge(flag_ready, 1)
            eps_matters = dve.value_load(eps_flag[0:1, 0:1], min_val=0, max_val=1)

            def damping(a, jb, t, f, r):
                with dve.If(eps_matters == 1):
                    dve.wait_ge(norm_bc_loaded, 16)
                    dve.wait_ge(score_done, t + 1)
                    n_i = norm_bc[:, a * GW:(a + 1) * GW]
                    n_j = norm[:, bass.ds(jb, 1)]
                    dve.tensor_scalar(damp[:, 0, :], n_i, n_j, COS_EPS, ALU.mult, ALU.add).then_inc(damp_step, 1)
                    dve.wait_ge(damp_step, f * 3 + 1)
                    dve.reciprocal(damp[:, 1, :], damp[:, 0, :]).then_inc(damp_step, 1)
                    dve.wait_ge(damp_step, f * 3 + 2)
                    dve.scalar_tensor_tensor(out=damp[:, 0, :], in0=n_i, scalar=n_j, in1=damp[:, 1, :],
                                             op0=ALU.mult, op1=ALU.mult).then_inc(damp_step, 1)
                    dve.wait_ge(damp_step, f * 3 + 3)
                    dve.tensor_tensor(score_ps(r), score_ps(r), damp[:, 0, :], ALU.mult).then_inc(score_damped, 1)

            def mask_direct(t, f, r, s, u, u_slot, loaded):
                dve.wait_ge(exp_ready, f + 1)
                dve.wait_ge(adj_loaded[u_slot], loaded)
                wait(dve, prob_hi_ready, t - GB + 1)
                wait(dve, mask_ready, u - 1)
                dve.scalar_tensor_tensor(out=prob[:, s, :], in0=adj_sb[:, u_slot, (s % 2) * GW:(s % 2 + 1) * GW], scalar=0.0,
                                         in1=expo[:, r, :], op0=ALU.is_gt, op1=ALU.mult).then_inc(prob_ready, 1)

            def mask_turned(t, s, u, u_slot, loaded):
                dve.wait_ge(score_done, t + 1)
                dve.wait_ge(adj_loaded[u_slot], loaded)
                wait(dve, prob_hi_ready, t - GB + 1)
                wait(dve, mask_ready, u - 1)
                dve.scalar_tensor_tensor(out=prob[:, s, :], in0=adj_sb[:, u_slot, (s % 2) * GW:(s % 2 + 1) * GW], scalar=0.0,
                                         in1=score_ps(s), op0=ALU.is_gt, op1=ALU.mult).then_inc(prob_ready, 1)

            def tails(t, s):
                dve.wait_ge(prob_hi_ready, t + 1)
                dve.wait_ge(prob_ready, t + 1)
                dve.scalar_tensor_tensor(out=prob_lo[:, s, :], in0=prob[:, s, :], scalar=PROB_SCALE, in1=prob_hi[:, s, :],
                                         op0=ALU.mult, op1=ALU.subtract).then_inc(prob_lo_ready, 1)

            def turned_out(a, b, h, t):
                wait_apart(dve, attn_done, t + 1, dve_passed)
                for u in range(2):
                    to = partial_of(b)[:, 2 * h + u, :]
                    if a == 0:
                        ins = dve.tensor_copy(to, turned_ps(u, D + 1))
                    else:
                        ins = dve.tensor_tensor(to, to, turned_ps(u, D + 1), ALU.add)
                    ins.then_inc(turned_copied, 1)

            def attention_out(a, t):
                dve.wait_ge(attn_done, t + 1)
                for q in range(GB):
                    dve.scalar_tensor_tensor(out=summed[:, q, 0:D + 1], in0=feat_hi[:, a * GB + q, 0:D + 1],
                                             scalar=diag_w[:, a * GB + q:a * GB + q + 1], in1=attn_ps(q, D + 1),
                                             op0=ALU.mult, op1=ALU.add).then_inc(attn_copied, 1)

            def softmax_scale(a):
                dve.wait_ge(attn_copied, (a + 1) * GB)
                if a:
                    chain.join(chain.step(dve.tensor_tensor(summed[:, :, 0:D + 1], summed[:, :, 0:D + 1], partial_of(a), ALU.add)))
                chain.join(chain.step(dve.reciprocal(rsum[:, :], summed[:, :, D])))
                chain.join(chain.step(dve.tensor_scalar(rsum_s[:, :], rsum[:, :], scales[:, 1:2], None, ALU.mult)))

            def residual_moments(a, q):
                chain.join(chain.step(dve.scalar_tensor_tensor(
                    out=summed[:, q, 0:D], in0=feat_lo[:, a * GB + q, :], scalar=diag_w[:, a * GB + q:a * GB + q + 1],
                    in1=summed[:, q, 0:D], op0=ALU.mult, op1=ALU.add)))
                if q == 0:
                    dve.wait_ge(xres_loaded, (a + 1) * 16)
                dve.scalar_tensor_tensor(out=summed[:, q, 0:D], in0=summed[:, q, 0:D], scalar=rsum_s[:, q:q + 1],
                                         in1=xres[:, q, :], op0=ALU.mult, op1=ALU.add).then_inc(summed_ready, 1)
                dve.wait_ge(summed_ready, a * GB + q + 1)
                chain.join(chain.step(dve.bn_stats(stats[:, q, :], summed[:, q, 0:D])))
                dve.bn_aggr(meanvar[:, q, :], stats[:, q, :]).then_inc(moments_ready, 1)

            def normalised(a, q):
                dve.wait_ge(rstd_ready, a * GB + q + 1)
                if q == 0:
                    wait(dve, x1_stored, a * 16)
                    dve.memset(x1_hi_of(a)[:, :, D:D + 1], 1.0).then_inc(x1_ones_ready, 1)
                chain.join(chain.step(dve.tensor_scalar(rows[:, q, :], summed[:, q, 0:D], meanvar[:, q, 0:1],
                                                        rstd[:, q:q + 1], ALU.subtract, ALU.mult)))
                chain.join(chain.step(dve.tensor_scalar(x1_hi_of(a)[:, q, 0:D], rows[:, q, :], NORM_SCALE, None, ALU.mult)))
                dve.scalar_tensor_tensor(out=x1_lo_of(a)[:, q, :], in0=rows[:, q, :], scalar=NORM_SCALE,
                                         in1=x1_hi_of(a)[:, q, 0:D], op0=ALU.mult, op1=ALU.subtract).then_inc(x1_ready, 1)

            def norm_work(a):
                pieces = [lambda: softmax_scale(a)]
                for q in range(GB):
                    pieces.append(lambda q=q: residual_moments(a, q))
                    if q:
                        pieces.append(lambda q=q: normalised(a, q - 1))
                pieces.append(lambda: normalised(a, GB - 1))
                return pieces

            def diagonal(a, between):
                t0, f0, u0 = tiles_before(a)
                for j in range(GB):
                    u = u0 + j // 2
                    if j == GB - 1 and a:
                        turned_out(a - 1, G - 1, 1, t0 - 1)
                    damping(a, a * GB + j, t0 + j, f0 + j, j)
                    mask_direct(t0 + j, f0 + j, j, j, u, u % 4, 16 * (u // 4 + 1))
                    if j:
                        tails(t0 + j - 1, j - 1)
                    if between and a:
                        between.pop(0)()
                tails(t0 + GB - 1, GB - 1)

            def pair(a, b, first, between):
                t0, f0, u0 = (before + more for before, more in zip(tiles_before(a), (GB, GB, 2)))
                n = b - a - 1
                tile = lambda j: n * STEP_TILES + (t0 + j)
                if a == 0:
                    split_features(b)
                for j in range(STEP_TILES):
                    u = u0 + j // 2
                    loaded = n * 16 + 16 * (u // 4 + 1)
                    if j == 3 and not first:
                        turned_out(a, b - 1, 1, tile(-1))
                    if j == 7:
                        turned_out(a, b, 0, tile(3))
                    if j in DIRECT:
                        r = DIRECT[j]
                        damping(a, b * GB + r, tile(j), n * GB + (f0 + r), r)
                        mask_direct(tile(j), n * GB + (f0 + r), r, j % GB, n * 4 + u, u % 4, loaded)
                    else:
                        mask_turned(tile(j), j % GB, n * 4 + u, u % 4, loaded)
                    if j:
                        tails(tile(j - 1), (j - 1) % GB)
                    if between:
                        between.pop(0)()
                tails(tile(STEP_TILES - 1), GB - 1)

            between = []
            for a in range(G):
                diagonal(a, between)
                unrolled = list(range(a + 1, G - 1))[:2 if a else 1]
                for b in unrolled:
                    pair(a, b, b == a + 1, between)
                if a + 1 + len(unrolled) < G - 1:
                    with dve.Fori(a + 1 + len(unrolled), G - 1) as b:
                        pair(a, b, False, None)
                if a < G - 1:
                    pair(a, G - 1, a == G - 2, between)
                for piece in between:
                    piece()
                last_direct = tiles_before(a + 1)[0] - (3 if a < G - 1 else 1)
                attention_out(a, last_direct)
                between = norm_work(a)
            for piece in between:
                piece()
            after_layer0 = chain.base + chain.count

            def invert_degree(b, slot):
                dve.wait_ge(agg_done, b + 1)
                wait(dve, agg_ready, b - 1)
                dve.tensor_scalar(deg[:, slot:slot + 1], agg_ps(slot, D + 1)[:, D:D + 1], 1.0, NORM_SCALE,
                                  ALU.max, ALU.mult).then_inc(deg_step, 1)
                dve.wait_ge(deg_step, b + 1)
                dve.reciprocal(rdeg[:, slot:slot + 1], deg[:, slot:slot + 1]).then_inc(rdeg_ready, 1)

            def dense_out(b, ig, q):
                steps = Steps(dve, dve_step, b * 2 + after_layer0)
                dve.wait_ge(dense_done, b + 1)
                dve.tensor_tensor(summed[:, q, 0:D], dense_ps(q % 2), bias_bc[:, :], ALU.add).then_inc(dense_read, 1)
                dve.wait_ge(dense_read, b + 1)
                dve.wait_ge(xb_loaded[q], (ig + 1) * 16)
                steps.join(steps.step(dve.scalar_tensor_tensor(
                    out=summed[:, q, 0:D], in0=summed[:, q, 0:D], scalar=0.0, in1=xres[:, q, :], op0=ALU.max, op1=ALU.add)))
                wait_apart(dve, dve_step, steps.step(dve.bn_stats(stats[:, q, :], summed[:, q, 0:D])), dve_passed)
                dve.bn_aggr(meanvar[:, q, :], stats[:, q, :]).then_inc(moments_ready, 1)

            def finish(b, ig, q):
                dve.wait_ge(rstd_ready, NB + b + 1)
                wait(dve, y_stored[q], ig * 16)
                dve.tensor_scalar(rows[:, q, :], summed[:, q, 0:D], meanvar[:, q, 0:1], rstd[:, q:q + 1],
                                  ALU.subtract, ALU.mult).then_inc(y_ready, 1)

            dve.wait_ge(setup_copied, 3)
            dve.wait_ge(x1_stored, 16 * G)

            def layer1_group(ig, first):
                for q in range(GB):
                    b = ig * GB + q
                    invert_degree(b, q % 2)
                    if q:
                        finish(b - 1, ig, q - 1)
                    elif not first:
                        finish(b - 1, ig - 1, GB - 1)
                    dense_out(b, ig, q)

            layer1_group(0, True)
            with dve.Fori(1, G) as ig:
                layer1_group(ig, False)
            finish(NB - 1, G - 1, GB - 1)

        @block.tensor
        def _(pe):
            def project(g):
                pe.wait_ge(xT_loaded[g % 4], 16 * (g // 4 + 1))
                wait(pe, wh_copied, g - 1)
                for b in range(GB):
                    for k in range(KD):
                        ins = pe.matmul(wh_ps(g % 2, b), xT_sb[:, g % 4, k, b * P:(b + 1) * P], w0T_sb[:, k, :],
                                        start=(k == 0), stop=(k == KD - 1))
                ins.then_inc(wh_done, 1)

            def turn_units(g):
                pe.wait_ge(unit_ready, g + 1)
                wait(pe, unitT_hi_ready, g - 1)
                wait(pe, unitT_lo_ready, g - 1)
                for half in range(2):
                    for b in range(GB):
                        for k in range(KD):
                            ins = pe.transpose(unitT_ps(g % 2, half)[:, k, b * P:(b + 1) * P],
                                               unit[:, g % 2, half, b, k * P:(k + 1) * P], ident16[:, :])
                ins.then_inc(unitT_done, 1)

            pe.wait_ge(w0_loaded, 16)
            pe.wait_ge(consts_ready, 2)
            project(0)
            project(1)
            for g in range(G):
                if g + 2 < G:
                    project(g + 2)
                turn_units(g)
            pe.wait_ge(wh_copied, G)
            pe.wait_ge(unitT_hi_ready, G)
            pe.wait_ge(unitT_lo_ready, G)

            def direct_scores(a, jb, t, j):
                wait(pe, prob_ready, t - 1)
                src = bass.ds(jb * P, P)
                tgt = slice(a * GW, (a + 1) * GW)
                for k in range(KD):
                    pe.matmul(score_ps(j), unitT_hi[:, k, src], unitT_lo[:, k, tgt], start=(k == 0), stop=False)
                    pe.matmul(score_ps(j), unitT_hi[:, k, src], unitT_hi[:, k, tgt], start=False, stop=False)
                    ins = pe.matmul(score_ps(j), unitT_lo[:, k, src], unitT_hi[:, k, tgt], start=False, stop=(k == KD - 1))
                ins.then_inc(score_done, 1)

            direct_scores(0, 0, 0, 0)
            direct_scores(0, 1, 1, 1)

            pe.wait_ge(extremes_ready, 1)
            pe.transpose(ps[0:1, 5, 0:P], extremes[:, 0:1], ident[:, :])
            pe.transpose(ps[0:1, 5, P:2 * P], extremes[:, 1:2], ident[:, :])
            pe.transpose(ps[0:NB, 5, 2 * P:3 * P], norm[:, :], ident[:, :]).then_inc(extremes_turned, 1)

            pe.wait_ge(setup_loaded, 16 * 6)
            pe.wait_ge(bias_wide_ready, 1)
            for part, w in ((0, w_selfT_sb), (1, w_nbT_sb)):
                for h in range(KD):
                    for k in range(KD):
                        pe.matmul(ps[:, 2 + part, h * D:(h + 1) * D], w[:, k, h * P:(h + 1) * P],
                                  w_comb_sb[:, part * KD + k, :], start=(k == 0), stop=(k == KD - 1))
            for k in range(2 * KD):
                pe.matmul(ps[:, 4, 0:D], bias_wide[:, k, :], w_comb_sb[:, k, :], start=(k == 0), stop=False)
            pe.matmul(ps[:, 4, 0:D], ones[0:1, :], bias_comb[0:1, :], start=False, stop=True).then_inc(setup_done, 1)

            pe.wait_ge(scale_row_ready, 1)
            pe.matmul(ps[:, 5, 3 * P:3 * P + 2], ones[0:1, :], scale_row[0:1, 0:2], start=True, stop=True).then_inc(scales_done, 1)
            pe.wait_ge(scales_ready, 1)
            pe.wait_ge(setup_copied, 3)
            pe.wait_ge(norms_copied, 1)

            def turned_scores(t, j, h, qp, f):
                pe.wait_ge(exp_ready, f + 1)
                wait(pe, prob_ready, t - 1)
                for s in range(2):
                    for u in range(2):
                        ins = pe.transpose(score_ps(j)[:, (2 * s + u) * P:(2 * s + u + 1) * P],
                                           expo[:, 2 * h + u, (2 * qp + s) * P:(2 * qp + s + 1) * P], ident[:, :])
                ins.then_inc(score_done, 1)

            def add_up(acc, s, cols, jb, start, stop):
                pe.matmul(acc(D + 1), prob_hi[:, s, cols], feat_hi[:, jb, 0:D + 1], start=start, stop=False)
                pe.matmul(acc(D), prob_hi[:, s, cols], feat_lo[:, jb, :], start=False, stop=False)
                return pe.matmul(acc(D + 1), prob_lo[:, s, cols], feat_hi[:, jb, 0:D + 1], start=False, stop=stop)

            def attend_direct(a, jb, t, s, start, stop):
                pe.wait_ge(prob_lo_ready, t + 1)
                for q in range(GB):
                    if start:
                        wait(pe, attn_copied, (a - 1) * GB + q + 1)
                    ins = add_up(lambda w: attn_ps(q, w), s, slice(q * P, (q + 1) * P), jb, start, stop)
                ins.then_inc(attn_done, 1)

            def attend_turned(a, t, s, qp, copied):
                pe.wait_ge(prob_lo_ready, t + 1)
                if qp == 0:
                    wait(pe, turned_copied, copied)
                for r in range(2):
                    for u in range(2):
                        ins = add_up(lambda w: turned_ps(u, w), s, slice((2 * r + u) * P, (2 * r + u + 1) * P),
                                     a * GB + 2 * qp + r, qp == 0 and r == 0, qp == 1 and r == 1)
                ins.then_inc(attn_done, 1)

            def front(a, b, j):
                t0, f0, _ = tiles_before(a)
                if b is None:
                    direct_scores(a, a * GB + j, t0 + j, j)
                    return
                n = b - a - 1
                t = n * STEP_TILES + (t0 + GB + j)
                if j in DIRECT:
                    direct_scores(a, b * GB + DIRECT[j], t, j)
                else:
                    h, qp = TURNED[j]
                    turned_scores(t, j, h, qp, n * GB + (f0 + GB + 2 * h + 1))

            def ahead(a, b, j, last):
                size = GB if b is None else STEP_TILES
                if j + AHEAD < size:
                    front(a, b, j + AHEAD)
                elif b is None:
                    if a + 1 < G:
                        front(a, a + 1, j + AHEAD - size)
                elif not last:
                    front(a, b + 1, j + AHEAD - size)
                else:
                    front(a + 1, None, j + AHEAD - size)

            def diagonal(a):
                t0 = tiles_before(a)[0]
                if a == 0:
                    pe.wait_ge(feat_ready, 1)
                for j in range(GB):
                    ahead(a, None, j, False)
                    attend_direct(a, a * GB + j, t0 + j, j, j == 0, a == G - 1 and j == GB - 1)

            def pair(a, b, last):
                t0 = tiles_before(a)[0] + GB
                halves = 2 * sum(G - 1 - k for k in range(a))
                n = b - a - 1
                if a == 0:
                    pe.wait_ge(feat_ready, b + 1)
                for j in range(STEP_TILES):
                    ahead(a, b, j, last)
                    t = n * STEP_TILES + (t0 + j)
                    if j in DIRECT:
                        attend_direct(a, b * GB + DIRECT[j], t, j % GB, False, last and j == 5)
                    else:
                        h, qp = TURNED[j]
                        attend_turned(a, t, j % GB, qp, n * 4 + 2 * (halves + h))

            front(0, None, 2)
            for a in range(G):
                diagonal(a)
                if a == 0:
                    pair(0, 1, False)
                if a < G - 2:
                    with pe.Fori(max(a + 1, 2), G - 1) as b:
                        pair(a, b, False)
                if a < G - 1:
                    pair(a, G - 1, True)

            pe.wait_ge(prob_ready, G * NB)
            pe.wait_ge(turned_copied, G * (G - 1) * 2)
            pe.wait_ge(x1_ones_ready, G)

            def aggregate(pair, b, ig, q, slot, first, tail):
                if q == 0:
                    pe.wait_ge(mgroup_loaded[slot], pair * 16 + 16)
                if first:
                    if b == 0:
                        pe.wait_ge(attn_copied, NB)
                if not (isinstance(b, int) and b < 2):
                    wait_apart(pe, agg_ready, b - 1, pe_passed)
                for jb in range(NB):
                    if first and b == 0 and jb % GB == 0:
                        pe.wait_ge(x1_ready, jb + GB)
                    lhsT = mgroup[:, slot, jb * GW + q * P:jb * GW + (q + 1) * P]
                    pe.matmul(agg_ps(q % 2, D + 1), lhsT, x1_hi_of(jb // GB)[:, jb % GB, 0:D + 1], start=(jb == 0), stop=False)
                    ins = pe.matmul(agg_ps(q % 2, D), lhsT, x1_lo_of(jb // GB)[:, jb % GB, :], start=False, stop=(jb == NB - 1))
                    if jb == NB // 4 and tail is not None:
                        turn(*tail)
                    if jb == NB * 3 // 4 and tail is not None:
                        dense(*tail)
                ins.then_inc(agg_done, 1)

            def turn(b, ig, q):
                pe.wait_ge(agg_ready, b + 1)
                pe.wait_ge(xb_loaded[q], (ig + 1) * 16)
                wait(pe, tr_ready, b - 1)
                slot = q % 2
                for k in range(KD):
                    pe.transpose(tr_ps(slot)[:, k * P:(k + 1) * P], xres[:, q, k * P:(k + 1) * P], ident[:, :])
                for k in range(KD):
                    ins = pe.transpose(tr_ps(slot)[:, (KD + k) * P:(KD + k + 1) * P], agg[:, slot, k * P:(k + 1) * P], ident[:, :])
                ins.then_inc(tr_done, 1)

            def dense(b, ig, q):
                pe.wait_ge(tr_ready, b + 1)
                wait(pe, dense_read, b - 1)
                for k in range(2 * KD):
                    ins = pe.matmul(dense_ps(q % 2), trT[:, q % 2, k, :], mixw[:, k, :], start=(k == 0), stop=(k == 2 * KD - 1))
                ins.then_inc(dense_done, 1)

            def layer1_pair(pair, first):
                for half in range(2):
                    ig = pair * 2 + half
                    for q in range(GB):
                        b = ig * GB + q
                        if q:
                            tail = (b - 1, ig, q - 1)
                        elif first and half == 0:
                            tail = None
                        else:
                            tail = (b - 1, ig - 1, GB - 1)
                        aggregate(pair, b, ig, q, half, first, tail)

            layer1_pair(0, True)
            with pe.Fori(1, NPAIR) as pair:
                layer1_pair(pair, False)
            turn(NB - 1, G - 1, GB - 1)
            dense(NB - 1, G - 1, GB - 1)


def kernel(x, adj, L0_gnn_W, L1_gnn_W_self, L1_gnn_b_self, L1_gnn_W_nb, L1_gnn_b_nb, L1_gnn_W_comb, L1_gnn_b_comb):
    import numpy as np
    import concourse.bacc as bacc
    from concourse.bass_utils import run_bass_kernel_spmd

    arrays = {
        "xT": np.ascontiguousarray(np.asarray(x).T),
        "x": np.ascontiguousarray(np.asarray(x)),
        "adjT": np.ascontiguousarray(np.asarray(adj).T),
        "w0T": np.ascontiguousarray(np.asarray(L0_gnn_W).T),
        "w_selfT": np.ascontiguousarray(np.asarray(L1_gnn_W_self).T),
        "b_self": np.ascontiguousarray(np.asarray(L1_gnn_b_self)),
        "w_nbT": np.ascontiguousarray(np.asarray(L1_gnn_W_nb).T),
        "b_nb": np.ascontiguousarray(np.asarray(L1_gnn_b_nb)),
        "w_comb": np.ascontiguousarray(np.asarray(L1_gnn_W_comb)),
        "b_comb": np.ascontiguousarray(np.asarray(L1_gnn_b_comb)),
    }
    nc = bacc.Bacc("TRN2", target_bir_lowering=False, num_devices=1)
    args = [nc.dram_tensor(name, a.shape, mybir.dt.from_np(a.dtype), kind="ExternalInput").ap()
            for name, a in arrays.items()]
    out = nc.dram_tensor("out", (N, D), F32, kind="ExternalOutput").ap()
    gnn_program(nc, *args, out)
    r = run_bass_kernel_spmd(nc, [arrays], core_ids=[0])
    return r.results[0]["out"]
```

```python
from contextlib import ExitStack

import concourse.bass as bass
from concourse import mybir

F32, F16, F8, I32, U8 = (mybir.dt.float32, mybir.dt.float16, mybir.dt.float8e4, mybir.dt.int32,
                          mybir.dt.uint8)
ALU = mybir.AluOpType
ACT = mybir.ActivationFunctionType
AX = mybir.AxisListType

P = 128
N, D = 4096, 256
KD = D // P
NB = N // P
GB = 4
G = NB // GB
GW = GB * P
NPAIR = G // 2
HW = GW // 2
STEP_TILES = 2 * GB
DIRECT = {0: 0, 1: 1, 4: 2, 5: 3}
TURNED = {2: (0, 0), 3: (0, 1), 6: (1, 0), 7: (1, 1)}
MGROUP0_STEP = 4
AHEAD = 3
AUG = D + 2
COS_EPS = 1e-8
LN_EPS = 1e-5
UNIT_SCALE = 4096.0
PROB_SCALE = 4096.0
FEAT_RANGE = 16384.0
NORM_SCALE = 2048.0
EPS_MATTERS_BELOW = 0.5


def wait(engine, semaphore, value):
    if not (isinstance(value, int) and value <= 0):
        engine.wait_ge(semaphore, value)


def wait_apart(engine, semaphore, value, passed):
    wait(engine, semaphore, value)
    if not isinstance(value, int):
        engine.sem_inc(passed, 1)


def tiles_before(a):
    pairs = sum(G - 1 - k for k in range(a))
    return GB * a + STEP_TILES * pairs, GB * (a + pairs), (GB * a + STEP_TILES * pairs) // 2


class Steps:

    def __init__(self, engine, semaphore, base):
        self.engine, self.semaphore, self.base, self.count = engine, semaphore, base, 0

    def step(self, instruction):
        instruction.then_inc(self.semaphore, 1)
        self.count += 1
        return self.base + self.count

    def join(self, value):
        self.engine.wait_ge(self.semaphore, value)


def gnn_program(nc, xT, x, adjT, w0T, w_selfT, b_self, w_nbT, b_nb, w_comb, b_comb, out):
    mask_spill = nc.dram_tensor("mask_spill", [G, P, NB, GW], U8, kind="Internal").ap()
    x1_spill = nc.dram_tensor("x1_spill", [G, P, GB, D], F32, kind="Internal").ap()
    norm_row_dram = nc.dram_tensor("norm_row_dram", [NB, P], F32, kind="Internal").ap()

    xT_v = xT.rearrange("(k p) i -> p k i", p=P)
    x_v = x.rearrange("(g q p) d -> g p q d", q=GB, p=P)
    out_v = out.rearrange("(b p) d -> b p d", p=P)
    adjT_v = adjT.rearrange("(c s p) i -> c p s i", s=GB, p=P)
    adj_diag_v = bass.AP(adjT.tensor, 0, [[N + 1, P], [P * (N + 1), NB]])

    ctx = ExitStack()
    with ctx:
        def sb(name, shape, dt):
            return ctx.enter_context(nc.sbuf_tensor(name, shape, dt))

        def sem(name):
            return ctx.enter_context(nc.semaphore(name))

        big = sb("big", [P, G, GB * (AUG + D) // 2], F32)
        big16 = big[:, :, :].bitcast(F16)

        def wh_of(g):
            return big[:, g, 0:GB * D].rearrange("p (b d) -> p b d", d=D)

        def partial_of(g):
            return big[:, g, 0:GB * (D + 1)].rearrange("p (b d) -> p b d", d=D + 1)

        def x1_hi_of(g):
            return big16[:, g, 0:GB * AUG].rearrange("p (b d) -> p b d", d=AUG)

        def x1_lo_of(g):
            return big16[:, g, GB * AUG:GB * (AUG + D)].rearrange("p (b d) -> p b d", d=D)

        unitT_hi = sb("unitT_hi", [P, KD, N], F16)
        unitT_lo = sb("unitT_lo", [P, KD, N], F16)
        feat_hi = sb("feat_hi", [P, NB, AUG], F16)
        feat_lo = sb("feat_lo", [P, NB, D], F16)
        work = sb("work", [P, 8 * GW], F32)
        xT_sb = feat_lo[:, :, :].bitcast(F32).rearrange("p b d -> p (b d)").rearrange("p (r k i) -> p r k i", r=4, k=KD)
        unit = work[:, 4 * GW:8 * GW].bitcast(F16).rearrange("p (r h b d) -> p r h b d", r=2, h=2, b=GB)
        expo = work[:, 0:4 * GW].rearrange("p (r i) -> p r i", r=GB)
        prob = work[:, 4 * GW:8 * GW].rearrange("p (r i) -> p r i", r=GB)
        prob_hi = sb("prob_hi", [P, GB, GW], F16)
        prob_lo = sb("prob_lo", [P, GB, GW], F16)
        adj_sb = sb("adj_sb", [P, 4, 2 * GW], I32)
        mask = sb("mask", [P, 4, 2 * GW], F8)
        mgroup = sb("mgroup", [P, 2, NB * GW], F8)
        setup_w = mgroup[:, 0, :].bitcast(F32)
        w_selfT_sb = setup_w[:, 0:KD * D].rearrange("p (k n) -> p k n", k=KD)
        w_nbT_sb = setup_w[:, KD * D:2 * KD * D].rearrange("p (k n) -> p k n", k=KD)
        w_comb_sb = setup_w[:, 2 * KD * D:4 * KD * D].rearrange("p (k n) -> p k n", k=2 * KD)
        norm_bc = mgroup[:, 1, :].bitcast(F32)
        w0T_sb = sb("w0T_sb", [P, KD, D], F32)
        mixw = sb("mixw", [P, 2 * KD, D], F32)
        bias_col = sb("bias_col", [P, 2 * KD], F32)
        agg_rows = sb("agg_rows", [P, 2 * D], F32)
        agg = agg_rows[:, :].rearrange("p (r d) -> p r d", r=2)
        bias_wide = agg_rows[:, :].rearrange("p (k m) -> p k m", k=2 * KD)
        bias_comb = sb("bias_comb", [1, D], F32)
        bias_bc = sb("bias_bc", [P, D], F32)
        ident = sb("ident", [P, P], F32)
        ident16 = sb("ident16", [P, P], F16)
        ones = sb("ones", [P, P], F32)
        xres = sb("xres", [P, GB, D], F32)
        rows = sb("rows", [P, GB, D], F32)
        summed = sb("summed", [P, GB, AUG], F32)
        trT = sb("trT", [P, 2, 2 * KD, P], F32)
        damp = trT[:, :, :, :].rearrange("p r k i -> p r (k i)")
        nsq = sb("nsq", [P, NB], F32)
        nsq_safe = sb("nsq_safe", [P, NB], F32)
        unit_mul = sb("unit_mul", [P, NB], F32)
        rnorm = sb("rnorm", [P, NB], F32)
        norm = sb("norm", [P, NB], F32)
        norm_row = sb("norm_row", [NB, P], F32)
        adj_diag = sb("adj_diag", [P, NB], I32)
        diag_a = sb("diag_a", [P, NB], F32)
        diag_b = sb("diag_b", [P, NB], F32)
        diag_e = sb("diag_e", [P, NB], F32)
        diag_w = sb("diag_w", [P, NB], F32)
        minus_half = sb("minus_half", [P, GB], F32)
        tiny = sb("tiny", [P, GB], F32)
        unit_scale = sb("unit_scale", [P, GB], F32)
        ln_eps = sb("ln_eps", [P, 1], F32)
        extremes = sb("extremes", [P, 2], F32)
        scale_row = sb("scale_row", [1, 4], F32)
        scales = sb("scales", [P, 2], F32)
        eps_flag = sb("eps_flag", [1, 1], I32)
        rsum = sb("rsum", [P, GB], F32)
        rsum_s = sb("rsum_s", [P, GB], F32)
        stats = sb("stats", [P, GB, 6], F32)
        meanvar = sb("meanvar", [P, GB, 2], F32)
        var_eps = sb("var_eps", [P, GB], F32)
        rstd = sb("rstd", [P, GB], F32)
        deg = sb("deg", [P, GB], F32)
        rdeg = sb("rdeg", [P, GB], F32)

        ps = ctx.enter_context(nc.psum_tensor("ps", [P, 8, GW], F32))

        def wh_ps(slot, b):
            return ps[:, 2 * slot + b // 2, (b % 2) * D:(b % 2 + 1) * D]

        def unitT_ps(slot, half):
            return ps[:, 4 + 2 * half + slot, :].bitcast(F16).rearrange("p (k i) -> p k i", k=KD)

        def score_ps(tile):
            return ps[:, tile % 2, :]

        def turned_ps(u, width):
            return ps[:, 2 + u, 0:width]

        def attn_ps(q, width):
            return ps[:, 4 + q, 0:width]

        def agg_ps(q, width):
            return ps[:, (2 + q) % 4, 0:width]

        def tr_ps(slot):
            return ps[:, 6 + slot, :]

        def dense_ps(slot):
            return ps[:, 4 + slot, 0:D]

        sync_passed, act_passed, dve_passed = sem("sync_passed"), sem("act_passed"), sem("dve_passed")
        pe_passed, pool_passed = sem("pe_passed"), sem("pool_passed")
        w0_loaded = sem("w0_loaded")
        xT_loaded = [sem(f"xT_loaded{i}") for i in range(4)]
        setup_loaded = sem("setup_loaded")
        diag_loaded = sem("diag_loaded")
        consts_cleared = sem("consts_cleared")
        consts_ready = sem("consts_ready")
        ones_ready = sem("ones_ready")
        wh_done = sem("wh_done")
        nsq_ready = sem("nsq_ready")
        wh_copied = sem("wh_copied")
        pool_step = sem("pool_step")
        norm_ready = sem("norm_ready")
        unit_hi_ready = sem("unit_hi_ready")
        unit_ready = sem("unit_ready")
        unitT_done = sem("unitT_done")
        unitT_hi_ready = sem("unitT_hi_ready")
        unitT_lo_ready = sem("unitT_lo_ready")
        bias_wide_ready = sem("bias_wide_ready")
        setup_done = sem("setup_done")
        setup_copied = sem("setup_copied")
        extremes_ready = sem("extremes_ready")
        extremes_turned = sem("extremes_turned")
        norms_copied = sem("norms_copied")
        norm_row_stored = sem("norm_row_stored")
        norm_bc_loaded = sem("norm_bc_loaded")
        scale_row_ready = sem("scale_row_ready")
        scales_done = sem("scales_done")
        scales_ready = sem("scales_ready")
        flag_ready = sem("flag_ready")
        diag_arg_ready = sem("diag_arg_ready")
        diag_exp_ready = sem("diag_exp_ready")
        feat_ready = sem("feat_ready")
        adj_loaded = [sem(f"adj_loaded{i}") for i in range(4)]
        mask_ready = sem("mask_ready")
        mask_stored = [sem(f"mask_stored{i}") for i in range(4)]
        score_done = sem("score_done")
        score_damped = sem("score_damped")
        exp_ready = sem("exp_ready")
        prob_ready = sem("prob_ready")
        prob_hi_ready = sem("prob_hi_ready")
        prob_lo_ready = sem("prob_lo_ready")
        attn_done = sem("attn_done")
        turned_copied = sem("turned_copied")
        attn_copied = sem("attn_copied")
        xres_loaded = sem("xres_loaded")
        moments_ready = sem("moments_ready")
        rstd_ready = sem("rstd_ready")
        x1_ready = sem("x1_ready")
        x1_stored = sem("x1_stored")
        feat_hi_step = sem("feat_hi_step")
        x1_ones_ready = sem("x1_ones_ready")
        summed_ready = sem("summed_ready")
        rows_ready = sem("rows_ready")
        deg_step = sem("deg_step")
        dve_step = sem("dve_step")
        damp_step = sem("damp_step")
        mgroup_loaded = [sem(f"mgroup_loaded{i}") for i in range(2)]
        xb_loaded = [sem(f"xb_loaded{i}") for i in range(GB)]
        agg_done = sem("agg_done")
        rdeg_ready = sem("rdeg_ready")
        agg_ready = sem("agg_ready")
        tr_done = sem("tr_done")
        tr_ready = sem("tr_ready")
        dense_done = sem("dense_done")
        dense_read = sem("dense_read")
        y_ready = sem("y_ready")
        y_stored = [sem(f"y_stored{i}") for i in range(GB)]

        block = ctx.enter_context(nc.Block())
        PHASE0_POOL = G * 3

        @block.sync
        def _(sync):
            def load_xT(g):
                sync.dma_start(xT_sb[:, g % 4], xT_v[:, :, g * GW:(g + 1) * GW]).then_inc(xT_loaded[g % 4], 16)

            sync.dma_start(w0T_sb[:, :, :], w0T.rearrange("(k p) n -> p k n", p=P)).then_inc(w0_loaded, 16)
            for g in range(4):
                load_xT(g)

            def load_direct(a, b, m, slot):
                sync.dma_start(adj_sb[:, slot, :].rearrange("p (s i) -> p s i", s=2),
                               adjT_v[b, :, 2 * m:2 * m + 2, a * GW:(a + 1) * GW]).then_inc(adj_loaded[slot], 16)

            def load_turned(a, b, h, slot):
                sync.dma_start(adj_sb[:, slot, :].rearrange("p (s i) -> p s i", s=GB),
                               adjT_v[a, :, :, bass.ds(b * GW + h * HW, HW)]).then_inc(adj_loaded[slot], 16)

            def load_unit(a, b, m, slot):
                if m % 2 == 0:
                    load_direct(a, b, m // 2, slot)
                else:
                    load_turned(a, b, m // 2, slot)

            def store_direct(a, b, m, slot):
                sync.dma_start(mask_spill[a, :, bass.ds(b * GB + 2 * m, 2), :],
                               mask[:, slot, :].bitcast(U8).rearrange("p (s i) -> p s i", s=2)).then_inc(mask_stored[slot], 16)

            def store_turned(a, b, h, slot):
                sync.dma_start(mask_spill[b, :, a * GB:(a + 1) * GB, h * HW:(h + 1) * HW],
                               mask[:, slot, :].bitcast(U8).rearrange("p (s i) -> p s i", s=GB)).then_inc(mask_stored[slot], 16)

            load_direct(0, 0, 0, 0)
            load_direct(0, 0, 1, 1)
            sync.dma_start(w_selfT_sb, w_selfT.rearrange("(k p) n -> p k n", p=P)).then_inc(setup_loaded, 16)
            sync.dma_start(w_nbT_sb, w_nbT.rearrange("(k p) n -> p k n", p=P)).then_inc(setup_loaded, 16)
            sync.dma_start(w_comb_sb, w_comb.rearrange("(k p) n -> p k n", p=P)).then_inc(setup_loaded, 16)
            with nc.allow_non_contiguous_dma(reason="biases as columns, the diagonal: single elements"):
                sync.dma_start(bias_col[:, 0:KD], b_self.rearrange("(k p) -> p k", p=P)).then_inc(setup_loaded, 16)
                sync.dma_start(bias_col[:, KD:2 * KD], b_nb.rearrange("(k p) -> p k", p=P)).then_inc(setup_loaded, 16)
                sync.dma_start(bias_comb[:, :], b_comb.rearrange("(a n) -> a n", a=1)).then_inc(setup_loaded, 16)
                sync.dma_start(adj_diag[:, :], adj_diag_v).then_inc(diag_loaded, 16)

            for g in range(4, G):
                sync.wait_ge(wh_done, g - 3)
                load_xT(g)
            load_unit(0, 1, 0, 2)
            load_unit(0, 1, 1, 3)
            sync.wait_ge(norms_copied, 1)
            sync.dma_start(norm_row_dram[:, :], norm_row[:, :]).then_inc(norm_row_stored, 16)
            sync.wait_ge(norm_row_stored, 16)
            sync.dma_start(norm_bc, norm_row_dram.rearrange("b p -> (b p)").partition_broadcast(P)).then_inc(norm_bc_loaded, 16)

            def diagonal(a):
                t0, _, u0 = tiles_before(a)
                for m in range(2):
                    slot = (u0 + m) % 4
                    if a + 1 < G:
                        sync.wait_ge(prob_ready, t0 + 2 * m + 2)
                        load_unit(a, a + 1, m + 2, slot)
                    sync.wait_ge(mask_ready, u0 + m + 1)
                    store_direct(a, a, m, slot)

            def pair(a, b, last):
                t0, u0 = tiles_before(a)[0] + GB, tiles_before(a)[2] + 2
                for m in range(4):
                    slot = (u0 + m) % 4
                    wait_apart(sync, prob_ready, (b - a - 1) * STEP_TILES + (t0 + 2 * m + 2), sync_passed)
                    if not last:
                        load_unit(a, b + 1, m, slot)
                    elif m < 2:
                        load_direct(a + 1, a + 1, m, slot)
                    elif a + 2 < G:
                        load_unit(a + 1, a + 2, m - 2, slot)
                    wait_apart(sync, mask_ready, (b - a - 1) * 4 + (u0 + m + 1), sync_passed)
                    if m % 2 == 0:
                        store_direct(a, b, m // 2, slot)
                    else:
                        store_turned(a, b, m // 2, slot)

            def load_mgroup(ig, slot):
                sync.dma_start(mgroup[:, slot, :].bitcast(U8), mask_spill[ig].rearrange("p b i -> p (b i)")).then_inc(mgroup_loaded[slot], 16)

            for a in range(G):
                diagonal(a)
                if a < G - 2:
                    with sync.Fori(a + 1, G - 1) as b:
                        pair(a, b, False)
                if a < G - 1:
                    pair(a, G - 1, True)
                if a:
                    sync.wait_ge(x1_ready, a * GB)
                    sync.dma_start(x1_spill[a - 1], rows[:, :, :]).then_inc(x1_stored, 16)
                sync.dma_start(xres[:, :, :], x_v[a]).then_inc(xres_loaded, 16)
                if a == MGROUP0_STEP:
                    for i in range(4):
                        sync.wait_ge(mask_stored[i], 16 * ((tiles_before(1)[2] + 3 - i) // 4))
                    sync.wait_ge(setup_done, 3)
                    load_mgroup(0, 0)

            for i in range(4):
                sync.wait_ge(mask_stored[i], 16 * (G * NB // 2 // 4))
            sync.wait_ge(norm_bc_loaded, 16)
            sync.wait_ge(prob_ready, NB * G)
            load_mgroup(1, 1)
            sync.wait_ge(x1_ready, NB)
            sync.dma_start(x1_spill[G - 1], rows[:, :, :]).then_inc(x1_stored, 16)
            sync.wait_ge(x1_stored, 16 * G)

            def load_xb(ig, q):
                sync.dma_start(xres[:, q, :], x1_spill[ig, :, q, :]).then_inc(xb_loaded[q], 16)

            for q in range(GB):
                load_xb(0, q)

            def finish(ig, slot, last_pair):
                for q in range(GB):
                    wait_apart(sync, y_ready, ig * GB + q + 1, sync_passed)
                    sync.dma_start(out_v[ig * GB + q], rows[:, q, :]).then_inc(y_stored[q], 16)
                    if not (last_pair and slot == 1):
                        load_xb(ig + 1, q)
                if not last_pair:
                    load_mgroup(ig + 2, slot)

            with sync.Fori(0, NPAIR - 1) as pair:
                finish(pair * 2, 0, False)
                finish(pair * 2 + 1, 1, False)
            finish(G - 2, 0, True)
            finish(G - 1, 1, True)
            for q in range(GB):
                sync.wait_ge(y_stored[q], 16 * G)

        @block.gpsimd
        def _(pool):
            pool.memset(ident[:, :], 0.0).then_inc(consts_cleared, 1)
            pool.memset(ident16[:, :], 0.0).then_inc(consts_cleared, 1)
            pool.memset(ones[:, :], 1.0).then_inc(ones_ready, 1)
            pool.memset(tiny[:, :], 1e-36)
            pool.memset(unit_scale[:, :], UNIT_SCALE)
            pool.memset(ln_eps[:, :], LN_EPS)
            pool.memset(minus_half[:, :], -0.5).then_inc(ones_ready, 1)
            pool.wait_ge(consts_cleared, 2)
            for m in (ident, ident16):
                pool.affine_select(out=m[:, :], in_=m[:, :], compare_op=ALU.not_equal, fill=1.0, base=0,
                                   pattern=[[-1, P]], channel_multiplier=1).then_inc(consts_ready, 1)
            pool.wait_ge(ones_ready, 2)

            def norms(g):
                cols = slice(g * GB, (g + 1) * GB)
                pool.wait_ge(nsq_ready, g + 1)
                pool.tensor_tensor(nsq_safe[:, cols], nsq[:, cols], tiny[:, :], ALU.add).then_inc(pool_step, 1)
                pool.wait_ge(pool_step, g * 3 + 1)
                pool.tensor_tensor(rnorm[:, cols], nsq_safe[:, cols], minus_half[:, :], ALU.pow).then_inc(pool_step, 1)
                pool.wait_ge(pool_step, g * 3 + 2)
                pool.tensor_tensor(norm[:, cols], nsq[:, cols], rnorm[:, cols], ALU.mult).then_inc(pool_step, 1)
                pool.wait_ge(pool_step, g * 3 + 3)
                pool.tensor_tensor(unit_mul[:, cols], rnorm[:, cols], unit_scale[:, :], ALU.mult).then_inc(norm_ready, 1)

            for g in range(G):
                norms(g)

            def inv_std(b, q):
                pool.wait_ge(moments_ready, b + 1)
                pool.tensor_tensor(var_eps[:, q:q + 1], meanvar[:, q, 1:2], ln_eps[:, :], ALU.add).then_inc(pool_step, 1)
                pool.wait_ge(pool_step, PHASE0_POOL + 1 + b)
                pool.tensor_tensor(rstd[:, q:q + 1], var_eps[:, q:q + 1], minus_half[:, 0:1], ALU.pow).then_inc(rstd_ready, 1)

            with pool.Fori(0, 2 * G) as ig:
                for q in range(GB):
                    inv_std(ig * GB + q, q)

        @block.scalar
        def _(act):
            def squares(g):
                act.wait_ge(wh_copied, g + 1)
                wait(act, nsq_ready, g)
                for b in range(GB):
                    ins = act.activation(rows[:, b, :], wh_of(g)[:, b, :], ACT.Square,
                                         accum_out=nsq[:, g * GB + b:g * GB + b + 1])
                ins.then_inc(nsq_ready, 1)

            def unitT_out(g):
                act.wait_ge(unitT_done, g + 1)
                act.activation(unitT_hi[:, :, g * GW:(g + 1) * GW], unitT_ps(g % 2, 0), ACT.Copy).then_inc(unitT_hi_ready, 1)

            def unit_heads(g):
                act.wait_ge(norm_ready, g + 1)
                wait(act, unitT_done, g - 1)
                for b in range(GB):
                    ins = act.activation(unit[:, g % 2, 0, b, :], wh_of(g)[:, b, :], ACT.Copy,
                                         scale=unit_mul[:, g * GB + b:g * GB + b + 1])
                ins.then_inc(unit_hi_ready, 1)

            squares(0)
            squares(1)
            unit_heads(0)
            def setup_out(n, to, bank, width):
                act.wait_ge(setup_done, n + 1)
                act.activation(to, ps[:, bank, 0:width], ACT.Copy).then_inc(setup_copied, 1)

            for g in range(1, G):
                if g + 1 < G:
                    squares(g + 1)
                unit_heads(g)
                if g == G - 2:
                    setup_out(0, mixw[:, 0:KD, :].rearrange("p k n -> p (k n)"), 3, KD * D)
                if g == G - 1:
                    setup_out(1, mixw[:, KD:2 * KD, :].rearrange("p k n -> p (k n)"), 1, KD * D)
                unitT_out(g - 1)
            act.wait_ge(flag_ready, 1)
            eps_matters = act.value_load(eps_flag[0:1, 0:1], min_val=0, max_val=1)

            def exponentials(t, f, r, since):
                with act.If(eps_matters == 1):
                    wait_apart(act, score_damped, f + 1, act_passed)
                wait_apart(act, score_done, t + 1, act_passed)
                wait(act, prob_ready, t - since + 1)
                act.activation(expo[:, r, :], score_ps(r), ACT.Exp, scale=1.0 / (UNIT_SCALE * UNIT_SCALE)).then_inc(exp_ready, 1)

            def heads(t, s):
                act.wait_ge(prob_ready, t + 1)
                wait(act, attn_done, t - GB + 1)
                act.activation(prob_hi[:, s, :], prob[:, s, :], ACT.Copy, scale=PROB_SCALE).then_inc(prob_hi_ready, 1)

            def unit_mask(u_slot, s, stored):
                wait_apart(act, mask_stored[u_slot], stored, act_passed)
                act.activation(mask[:, u_slot, :], prob[:, s:s + 2, :].rearrange("p r i -> p (r i)"), ACT.Sign,
                               saturate=False).then_inc(mask_ready, 1)

            def diagonal(a):
                t0, f0, u0 = tiles_before(a)
                exponentials(t0, f0, 0, STEP_TILES)
                if a == 0:
                    unitT_out(G - 1)
                for j in range(GB):
                    if j + 1 < GB:
                        exponentials(t0 + j + 1, f0 + j + 1, j + 1, STEP_TILES if j == 0 else STEP_TILES - 2)
                    heads(t0 + j, j)
                    if j % 2:
                        u = u0 + j // 2
                        unit_mask(u % 4, j - 1, 16 * (u // 4))

            def pair(a, b):
                t0, f0, u0 = (first + more for first, more in zip(tiles_before(a), (GB, GB, 2)))
                n = b - a - 1
                tile = lambda j: n * STEP_TILES + (t0 + j)
                exponentials(tile(0), n * GB + f0, 0, GB)
                exponentials(tile(1), n * GB + (f0 + 1), 1, GB)
                for j in range(STEP_TILES):
                    if j == 2:
                        exponentials(tile(4), n * GB + (f0 + 2), 2, GB + 2)
                    heads(tile(j), j % GB)
                    if j == 3:
                        exponentials(tile(5), n * GB + (f0 + 3), 3, GB + 2)
                    if j % 2:
                        m = j // 2
                        unit_mask((u0 + m) % 4, (j - 1) % GB, n * 16 + 16 * ((u0 + m) // 4))

            for a in range(G):
                diagonal(a)
                if a == 0:
                    setup_out(2, bias_bc[:, :], 3, D)
                    act.wait_ge(diag_arg_ready, 1)
                    act.activation(diag_e[:, :], diag_a[:, :], ACT.Exp).then_inc(diag_exp_ready, 1)
                    pair(0, 1)
                if a < G - 2:
                    with act.Fori(max(a + 1, 2), G - 1) as b:
                        pair(a, b)
                if a < G - 1:
                    pair(a, G - 1)

            def mean_and_transposes(b, q):
                slot = q % 2
                act.wait_ge(agg_done, b + 1)
                act.wait_ge(rdeg_ready, b + 1)
                wait(act, tr_done, b - 1)
                act.activation(agg[:, slot, :], agg_ps(q, D), ACT.Copy, scale=rdeg[:, q:q + 1]).then_inc(agg_ready, 1)
                act.wait_ge(tr_done, b + 1)
                wait(act, dense_done, b - 1)
                act.activation(trT[:, slot].rearrange("p k i -> p (k i)"), tr_ps(slot), ACT.Copy).then_inc(tr_ready, 1)

            for q in range(GB):
                mean_and_transposes(q, q)
            with act.Fori(1, G) as ig:
                for q in range(GB):
                    mean_and_transposes(ig * GB + q, q)

        @block.vector
        def _(dve):
            def widen_biases():
                dve.wait_ge(setup_loaded, 16 * 6)
                dve.wait_ge(ones_ready, 2)
                for k in range(2 * KD):
                    ins = dve.tensor_scalar(bias_wide[:, k, :], ones[:, :], bias_col[:, k:k + 1], None, ALU.mult)
                ins.then_inc(bias_wide_ready, 1)

            def copy_wh(g):
                dve.wait_ge(wh_done, g + 1)
                dve.tensor_copy(wh_of(g).rearrange("p (a b) d -> p a (b d)", a=2),
                                ps[:, 2 * (g % 2):2 * (g % 2) + 2, :]).then_inc(wh_copied, 1)

            def unit_tails(g):
                dve.wait_ge(unit_hi_ready, g + 1)
                dve.wait_ge(wh_copied, g + 1)
                for b in range(GB):
                    ins = dve.scalar_tensor_tensor(out=unit[:, g % 2, 1, b, :], in0=wh_of(g)[:, b, :],
                                                   scalar=unit_mul[:, g * GB + b:g * GB + b + 1],
                                                   in1=unit[:, g % 2, 0, b, :], op0=ALU.mult, op1=ALU.subtract)
                ins.then_inc(unit_ready, 1)

            def unitT_out(g):
                dve.wait_ge(unitT_done, g + 1)
                dve.tensor_copy(unitT_lo[:, :, g * GW:(g + 1) * GW], unitT_ps(g % 2, 1)).then_inc(unitT_lo_ready, 1)

            chain = Steps(dve, dve_step, 0)
            copy_wh(0)
            copy_wh(1)
            for g in range(G):
                if g + 2 < G:
                    copy_wh(g + 2)
                if g < G - 1:
                    unit_tails(g)
                if g == 2:
                    widen_biases()
                if 0 < g < G - 1:
                    unitT_out(g - 1)

            dve.wait_ge(norm_ready, G)
            dve.reduce_max(extremes[:, 0:1], norm[:, :], AX.X)
            dve.tensor_reduce(extremes[:, 1:2], norm[:, :], AX.X, ALU.min).then_inc(extremes_ready, 1)
            dve.memset(feat_hi[:, :, D:D + 1], 1.0)
            dve.wait_ge(extremes_turned, 1)
            chain.join(chain.step(dve.reduce_max(scale_row[0:1, 2:3], ps[0:1, 2, 0:P], AX.X)))
            chain.join(chain.step(dve.tensor_scalar(scale_row[0:1, 1:2], scale_row[0:1, 2:3], 1e-30, 1.0 / FEAT_RANGE, ALU.max, ALU.mult)))
            dve.reciprocal(scale_row[0:1, 0:1], scale_row[0:1, 1:2]).then_inc(scale_row_ready, 1)
            chain.join(chain.step(dve.tensor_reduce(scale_row[0:1, 3:4], ps[0:1, 2, P:2 * P], AX.X, ALU.min)))
            dve.tensor_scalar(eps_flag[0:1, :], scale_row[0:1, 3:4], EPS_MATTERS_BELOW, None, ALU.is_lt).then_inc(flag_ready, 1)
            dve.tensor_copy(norm_row[:, :], ps[0:NB, 2, 2 * P:3 * P]).then_inc(norms_copied, 1)
            dve.wait_ge(scales_done, 1)
            dve.tensor_copy(scales[:, :], ps[:, 2, 3 * P:3 * P + 2]).then_inc(scales_ready, 1)
            unit_tails(G - 1)
            dve.wait_ge(scales_ready, 1)

            def split_features(g):
                grp = bass.ds(g * GB, GB)
                dve.tensor_scalar(feat_hi[:, grp, 0:D], wh_of(g), scales[:, 0:1], None, ALU.mult).then_inc(feat_hi_step, 1)
                dve.wait_ge(feat_hi_step, g + 1)
                dve.scalar_tensor_tensor(out=feat_lo[:, grp, :], in0=wh_of(g), scalar=scales[:, 0:1],
                                         in1=feat_hi[:, grp, 0:D], op0=ALU.mult, op1=ALU.subtract).then_inc(feat_ready, 1)

            split_features(0)
            unitT_out(G - 2)

            dve.wait_ge(flag_ready, 1)
            eps_matters = dve.value_load(eps_flag[0:1, 0:1], min_val=0, max_val=1)

            def diagonal_weights():
                chain.join(chain.step(dve.tensor_scalar(diag_b[:, :], nsq[:, :], COS_EPS, None, ALU.add)))
                chain.join(chain.step(dve.reciprocal(diag_w[:, :], diag_b[:, :])))
                dve.tensor_tensor(diag_a[:, :], nsq[:, :], diag_w[:, :], ALU.mult).then_inc(diag_arg_ready, 1)
                dve.wait_ge(diag_loaded, 16)
                chain.join(chain.step(dve.tensor_scalar(diag_b[:, :], adj_diag[:, :], 0.0, -PROB_SCALE, ALU.is_gt, ALU.mult)))
                dve.wait_ge(diag_exp_ready, 1)
                chain.join(chain.step(dve.scalar_tensor_tensor(out=diag_w[:, :], in0=diag_b[:, :], scalar=PROB_SCALE,
                                                               in1=diag_e[:, :], op0=ALU.add, op1=ALU.mult)))

            def damping(a, jb, t, f, r):
                with dve.If(eps_matters == 1):
                    dve.wait_ge(norm_bc_loaded, 16)
                    dve.wait_ge(score_done, t + 1)
                    n_i = norm_bc[:, a * GW:(a + 1) * GW]
                    n_j = norm[:, bass.ds(jb, 1)]
                    dve.tensor_scalar(damp[:, 0, :], n_i, n_j, COS_EPS, ALU.mult, ALU.add).then_inc(damp_step, 1)
                    dve.wait_ge(damp_step, f * 3 + 1)
                    dve.reciprocal(damp[:, 1, :], damp[:, 0, :]).then_inc(damp_step, 1)
                    dve.wait_ge(damp_step, f * 3 + 2)
                    dve.scalar_tensor_tensor(out=damp[:, 0, :], in0=n_i, scalar=n_j, in1=damp[:, 1, :],
                                             op0=ALU.mult, op1=ALU.mult).then_inc(damp_step, 1)
                    dve.wait_ge(damp_step, f * 3 + 3)
                    dve.tensor_tensor(score_ps(r), score_ps(r), damp[:, 0, :], ALU.mult).then_inc(score_damped, 1)

            def mask_direct(t, f, r, s, u, u_slot, loaded):
                dve.wait_ge(exp_ready, f + 1)
                dve.wait_ge(adj_loaded[u_slot], loaded)
                wait(dve, prob_hi_ready, t - GB + 1)
                wait(dve, mask_ready, u - 1)
                dve.scalar_tensor_tensor(out=prob[:, s, :], in0=adj_sb[:, u_slot, (s % 2) * GW:(s % 2 + 1) * GW], scalar=0.0,
                                         in1=expo[:, r, :], op0=ALU.is_gt, op1=ALU.mult).then_inc(prob_ready, 1)

            def mask_turned(t, s, u, u_slot, loaded):
                dve.wait_ge(score_done, t + 1)
                dve.wait_ge(adj_loaded[u_slot], loaded)
                wait(dve, prob_hi_ready, t - GB + 1)
                wait(dve, mask_ready, u - 1)
                dve.scalar_tensor_tensor(out=prob[:, s, :], in0=adj_sb[:, u_slot, (s % 2) * GW:(s % 2 + 1) * GW], scalar=0.0,
                                         in1=score_ps(s), op0=ALU.is_gt, op1=ALU.mult).then_inc(prob_ready, 1)

            def tails(t, s):
                dve.wait_ge(prob_hi_ready, t + 1)
                dve.wait_ge(prob_ready, t + 1)
                dve.scalar_tensor_tensor(out=prob_lo[:, s, :], in0=prob[:, s, :], scalar=PROB_SCALE, in1=prob_hi[:, s, :],
                                         op0=ALU.mult, op1=ALU.subtract).then_inc(prob_lo_ready, 1)

            def turned_out(a, b, h, t):
                wait_apart(dve, attn_done, t + 1, dve_passed)
                for u in range(2):
                    to = partial_of(b)[:, 2 * h + u, :]
                    if a == 0:
                        ins = dve.tensor_copy(to, turned_ps(u, D + 1))
                    else:
                        ins = dve.tensor_tensor(to, to, turned_ps(u, D + 1), ALU.add)
                    ins.then_inc(turned_copied, 1)

            def attention_out(a, t):
                dve.wait_ge(attn_done, t + 1)
                for q in range(GB):
                    dve.scalar_tensor_tensor(out=summed[:, q, 0:D + 1], in0=feat_hi[:, a * GB + q, 0:D + 1],
                                             scalar=diag_w[:, a * GB + q:a * GB + q + 1], in1=attn_ps(q, D + 1),
                                             op0=ALU.mult, op1=ALU.add).then_inc(attn_copied, 1)

            def softmax_scale(a):
                dve.wait_ge(attn_copied, (a + 1) * GB)
                if a:
                    chain.join(chain.step(dve.tensor_tensor(summed[:, :, 0:D + 1], summed[:, :, 0:D + 1], partial_of(a), ALU.add)))
                chain.join(chain.step(dve.reciprocal(rsum[:, :], summed[:, :, D])))
                chain.join(chain.step(dve.tensor_scalar(rsum_s[:, :], rsum[:, :], scales[:, 1:2], None, ALU.mult)))

            def residual(a, q):
                chain.join(chain.step(dve.scalar_tensor_tensor(
                    out=summed[:, q, 0:D], in0=feat_lo[:, a * GB + q, :], scalar=diag_w[:, a * GB + q:a * GB + q + 1],
                    in1=summed[:, q, 0:D], op0=ALU.mult, op1=ALU.add)))
                if q == 0:
                    dve.wait_ge(xres_loaded, (a + 1) * 16)
                dve.scalar_tensor_tensor(out=summed[:, q, 0:D], in0=summed[:, q, 0:D], scalar=rsum_s[:, q:q + 1],
                                         in1=xres[:, q, :], op0=ALU.mult, op1=ALU.add).then_inc(summed_ready, 1)

            def moments(a, q):
                dve.wait_ge(summed_ready, a * GB + q + 1)
                chain.join(chain.step(dve.bn_stats(stats[:, q, :], summed[:, q, 0:D])))
                dve.bn_aggr(meanvar[:, q, :], stats[:, q, :]).then_inc(moments_ready, 1)

            def normalised(a, q):
                dve.wait_ge(rstd_ready, a * GB + q + 1)
                if q == 0:
                    wait(dve, x1_stored, a * 16)
                    dve.memset(x1_hi_of(a)[:, :, D:D + 1], 1.0).then_inc(x1_ones_ready, 1)
                dve.tensor_scalar(rows[:, q, :], summed[:, q, 0:D], meanvar[:, q, 0:1],
                                  rstd[:, q:q + 1], ALU.subtract, ALU.mult).then_inc(rows_ready, 1)

            def split_x1(a, q):
                dve.wait_ge(rows_ready, a * GB + q + 1)
                chain.join(chain.step(dve.tensor_scalar(x1_hi_of(a)[:, q, 0:D], rows[:, q, :], NORM_SCALE, None, ALU.mult)))
                dve.scalar_tensor_tensor(out=x1_lo_of(a)[:, q, :], in0=rows[:, q, :], scalar=NORM_SCALE,
                                         in1=x1_hi_of(a)[:, q, 0:D], op0=ALU.mult, op1=ALU.subtract).then_inc(x1_ready, 1)

            def norm_work(a):
                pieces = [lambda: softmax_scale(a)]
                for q in range(GB + 1):
                    if q < GB:
                        pieces.append(lambda q=q: residual(a, q))
                        pieces.append(lambda q=q: moments(a, q))
                    if q:
                        pieces.append(lambda q=q: normalised(a, q - 1))
                        pieces.append(lambda q=q: split_x1(a, q - 1))
                return pieces

            def diagonal(a, between):
                t0, f0, u0 = tiles_before(a)
                for j in range(GB):
                    u = u0 + j // 2
                    if j == GB - 1 and a:
                        turned_out(a - 1, G - 1, 1, t0 - 1)
                    damping(a, a * GB + j, t0 + j, f0 + j, j)
                    mask_direct(t0 + j, f0 + j, j, j, u, u % 4, 16 * (u // 4 + 1))
                    if a == 0 and j == 0:
                        unitT_out(G - 1)
                    if j:
                        tails(t0 + j - 1, j - 1)
                    if between and 0 < a < G - 1 and j < GB - 1:
                        between.pop(0)()
                tails(t0 + GB - 1, GB - 1)

            def pair(a, b, first, between):
                t0, f0, u0 = (before + more for before, more in zip(tiles_before(a), (GB, GB, 2)))
                n = b - a - 1
                tile = lambda j: n * STEP_TILES + (t0 + j)
                if a == 0:
                    split_features(b)
                for j in range(STEP_TILES):
                    u = u0 + j // 2
                    loaded = n * 16 + 16 * (u // 4 + 1)
                    if j == 3 and not first:
                        turned_out(a, b - 1, 1, tile(-1))
                    if j == 7:
                        turned_out(a, b, 0, tile(3))
                    if j in DIRECT:
                        r = DIRECT[j]
                        damping(a, b * GB + r, tile(j), n * GB + (f0 + r), r)
                        mask_direct(tile(j), n * GB + (f0 + r), r, j % GB, n * 4 + u, u % 4, loaded)
                    else:
                        mask_turned(tile(j), j % GB, n * 4 + u, u % 4, loaded)
                    if j:
                        tails(tile(j - 1), (j - 1) % GB)
                    if between and j != 3:
                        between.pop(0)()
                        if a == G - 2:
                            between.pop(0)()
                tails(tile(STEP_TILES - 1), GB - 1)

            between = []
            for a in range(G):
                diagonal(a, between)
                if a == 0:
                    diagonal_weights()
                unrolled = list(range(a + 1, G - 1))[:2 if a else 1]
                for b in unrolled:
                    pair(a, b, b == a + 1, between)
                if a + 1 + len(unrolled) < G - 1:
                    with dve.Fori(a + 1 + len(unrolled), G - 1) as b:
                        pair(a, b, False, None)
                if a < G - 1:
                    pair(a, G - 1, a == G - 2, between)
                for piece in between:
                    piece()
                last_direct = tiles_before(a + 1)[0] - (3 if a < G - 1 else 1)
                attention_out(a, last_direct)
                between = norm_work(a)
            for piece in between:
                piece()
            after_layer0 = chain.base + chain.count

            def invert_degree(b, q):
                dve.wait_ge(agg_done, b + 1)
                wait(dve, agg_ready, b - GB + 1)
                dve.tensor_scalar(deg[:, q:q + 1], agg_ps(q, D + 1)[:, D:D + 1], 1.0, NORM_SCALE,
                                  ALU.max, ALU.mult).then_inc(deg_step, 1)
                dve.wait_ge(deg_step, b + 1)
                dve.reciprocal(rdeg[:, q:q + 1], deg[:, q:q + 1]).then_inc(rdeg_ready, 1)

            def dense_out(b, ig, q):
                steps = Steps(dve, dve_step, b * 2 + after_layer0)
                dve.wait_ge(dense_done, b + 1)
                dve.tensor_tensor(summed[:, q, 0:D], dense_ps(q % 2), bias_bc[:, :], ALU.add).then_inc(dense_read, 1)
                dve.wait_ge(dense_read, b + 1)
                dve.wait_ge(xb_loaded[q], (ig + 1) * 16)
                steps.join(steps.step(dve.scalar_tensor_tensor(
                    out=summed[:, q, 0:D], in0=summed[:, q, 0:D], scalar=0.0, in1=xres[:, q, :], op0=ALU.max, op1=ALU.add)))
                wait_apart(dve, dve_step, steps.step(dve.bn_stats(stats[:, q, :], summed[:, q, 0:D])), dve_passed)
                dve.bn_aggr(meanvar[:, q, :], stats[:, q, :]).then_inc(moments_ready, 1)

            def finish(b, ig, q):
                dve.wait_ge(rstd_ready, NB + b + 1)
                wait(dve, y_stored[q], ig * 16)
                dve.tensor_scalar(rows[:, q, :], summed[:, q, 0:D], meanvar[:, q, 0:1], rstd[:, q:q + 1],
                                  ALU.subtract, ALU.mult).then_inc(y_ready, 1)

            dve.wait_ge(setup_copied, 3)

            def layer1_group(ig, first):
                if first:
                    for q in range(GB):
                        invert_degree(q, q)
                for q in range(GB):
                    b = ig * GB + q
                    if not first:
                        invert_degree(b, q)
                    if first and q == 1:
                        dve.wait_ge(x1_stored, 16 * G)
                    if q:
                        finish(b - 1, ig, q - 1)
                    elif not first:
                        finish(b - 1, ig - 1, GB - 1)
                    dense_out(b, ig, q)

            layer1_group(0, True)
            with dve.Fori(1, G) as ig:
                layer1_group(ig, False)
            finish(NB - 1, G - 1, GB - 1)

        @block.tensor
        def _(pe):
            def project(g):
                pe.wait_ge(xT_loaded[g % 4], 16 * (g // 4 + 1))
                wait(pe, wh_copied, g - 1)
                for b in range(GB):
                    for k in range(KD):
                        ins = pe.matmul(wh_ps(g % 2, b), xT_sb[:, g % 4, k, b * P:(b + 1) * P], w0T_sb[:, k, :],
                                        start=(k == 0), stop=(k == KD - 1))
                ins.then_inc(wh_done, 1)

            def turn_units(g):
                pe.wait_ge(unit_ready, g + 1)
                wait(pe, unitT_hi_ready, g - 1)
                wait(pe, unitT_lo_ready, g - 1)
                for half in range(2):
                    for b in range(GB):
                        for k in range(KD):
                            ins = pe.transpose(unitT_ps(g % 2, half)[:, k, b * P:(b + 1) * P],
                                               unit[:, g % 2, half, b, k * P:(k + 1) * P], ident16[:, :])
                ins.then_inc(unitT_done, 1)

            pe.wait_ge(w0_loaded, 16)
            pe.wait_ge(consts_ready, 2)
            for g in range(4):
                project(g)
            for g in range(4):
                turn_units(g)
                project(g + 4)
            turn_units(4)

            def direct_scores(a, jb, t, j):
                wait(pe, prob_ready, t - 1)
                src = bass.ds(jb * P, P)
                tgt = slice(a * GW, (a + 1) * GW)
                for k in range(KD):
                    pe.matmul(score_ps(j), unitT_hi[:, k, src], unitT_lo[:, k, tgt], start=(k == 0), stop=False)
                    pe.matmul(score_ps(j), unitT_hi[:, k, src], unitT_hi[:, k, tgt], start=False, stop=False)
                    ins = pe.matmul(score_ps(j), unitT_lo[:, k, src], unitT_hi[:, k, tgt], start=False, stop=(k == KD - 1))
                ins.then_inc(score_done, 1)

            pe.wait_ge(wh_copied, G)
            pe.wait_ge(unitT_hi_ready, 1)
            pe.wait_ge(unitT_lo_ready, 1)
            direct_scores(0, 0, 0, 0)

            def combine(part, w, bank):
                for h in range(KD):
                    for k in range(KD):
                        ins = pe.matmul(ps[:, bank, h * D:(h + 1) * D], w[:, k, h * P:(h + 1) * P],
                                        w_comb_sb[:, part * KD + k, :], start=(k == 0), stop=(k == KD - 1))
                ins.then_inc(setup_done, 1)

            pe.wait_ge(setup_loaded, 16 * 6)
            combine(0, w_selfT_sb, 3)
            turn_units(5)
            combine(1, w_nbT_sb, 1)
            turn_units(6)

            pe.wait_ge(extremes_ready, 1)
            pe.transpose(ps[0:1, 2, 0:P], extremes[:, 0:1], ident[:, :])
            pe.transpose(ps[0:1, 2, P:2 * P], extremes[:, 1:2], ident[:, :])
            pe.transpose(ps[0:NB, 2, 2 * P:3 * P], norm[:, :], ident[:, :]).then_inc(extremes_turned, 1)

            pe.wait_ge(scale_row_ready, 1)
            pe.wait_ge(norms_copied, 1)
            pe.matmul(ps[:, 2, 3 * P:3 * P + 2], ones[0:1, :], scale_row[0:1, 0:2], start=True, stop=True).then_inc(scales_done, 1)
            pe.wait_ge(setup_copied, 2)
            direct_scores(0, 1, 1, 1)
            turn_units(7)

            pe.wait_ge(bias_wide_ready, 1)
            pe.wait_ge(setup_copied, 1)
            for k in range(2 * KD):
                pe.matmul(ps[:, 3, 0:D], bias_wide[:, k, :], w_comb_sb[:, k, :], start=(k == 0), stop=False)
            pe.matmul(ps[:, 3, 0:D], ones[0:1, :], bias_comb[0:1, :], start=False, stop=True).then_inc(setup_done, 1)

            pe.wait_ge(unitT_hi_ready, G)
            pe.wait_ge(unitT_lo_ready, G)
            pe.wait_ge(scales_ready, 1)

            def turned_scores(t, j, h, qp, f):
                pe.wait_ge(exp_ready, f + 1)
                wait(pe, prob_ready, t - 1)
                for s in range(2):
                    for u in range(2):
                        ins = pe.transpose(score_ps(j)[:, (2 * s + u) * P:(2 * s + u + 1) * P],
                                           expo[:, 2 * h + u, (2 * qp + s) * P:(2 * qp + s + 1) * P], ident[:, :])
                ins.then_inc(score_done, 1)

            def add_up(acc, s, cols, jb, start, stop):
                pe.matmul(acc(D + 1), prob_hi[:, s, cols], feat_hi[:, jb, 0:D + 1], start=start, stop=False)
                pe.matmul(acc(D), prob_hi[:, s, cols], feat_lo[:, jb, :], start=False, stop=False)
                return pe.matmul(acc(D + 1), prob_lo[:, s, cols], feat_hi[:, jb, 0:D + 1], start=False, stop=stop)

            def attend_direct(a, jb, t, s, start, stop):
                pe.wait_ge(prob_lo_ready, t + 1)
                for q in range(GB):
                    if start:
                        wait(pe, attn_copied, (a - 1) * GB + q + 1)
                    ins = add_up(lambda w: attn_ps(q, w), s, slice(q * P, (q + 1) * P), jb, start, stop)
                ins.then_inc(attn_done, 1)

            def attend_turned(a, t, s, qp, copied):
                pe.wait_ge(prob_lo_ready, t + 1)
                if qp == 0:
                    wait(pe, turned_copied, copied)
                for r in range(2):
                    for u in range(2):
                        ins = add_up(lambda w: turned_ps(u, w), s, slice((2 * r + u) * P, (2 * r + u + 1) * P),
                                     a * GB + 2 * qp + r, qp == 0 and r == 0, qp == 1 and r == 1)
                ins.then_inc(attn_done, 1)

            def front(a, b, j):
                t0, f0, _ = tiles_before(a)
                if b is None:
                    direct_scores(a, a * GB + j, t0 + j, j)
                    return
                n = b - a - 1
                t = n * STEP_TILES + (t0 + GB + j)
                if j in DIRECT:
                    direct_scores(a, b * GB + DIRECT[j], t, j)
                else:
                    h, qp = TURNED[j]
                    turned_scores(t, j, h, qp, n * GB + (f0 + GB + 2 * h + 1))

            def ahead(a, b, j, last):
                size = GB if b is None else STEP_TILES
                if j + AHEAD < size:
                    front(a, b, j + AHEAD)
                elif b is None:
                    if a + 1 < G:
                        front(a, a + 1, j + AHEAD - size)
                elif not last:
                    front(a, b + 1, j + AHEAD - size)
                else:
                    front(a + 1, None, j + AHEAD - size)

            def diagonal(a):
                t0 = tiles_before(a)[0]
                if a == 0:
                    pe.wait_ge(feat_ready, 1)
                for j in range(GB):
                    ahead(a, None, j, False)
                    attend_direct(a, a * GB + j, t0 + j, j, j == 0, a == G - 1 and j == GB - 1)

            def pair(a, b, last):
                t0 = tiles_before(a)[0] + GB
                halves = 2 * sum(G - 1 - k for k in range(a))
                n = b - a - 1
                if a == 0:
                    pe.wait_ge(feat_ready, b + 1)
                    if isinstance(b, int) and b == 1:
                        pe.wait_ge(setup_copied, 3)
                for j in range(STEP_TILES):
                    ahead(a, b, j, last)
                    t = n * STEP_TILES + (t0 + j)
                    if j in DIRECT:
                        attend_direct(a, b * GB + DIRECT[j], t, j % GB, False, last and j == 5)
                    else:
                        h, qp = TURNED[j]
                        attend_turned(a, t, j % GB, qp, n * 4 + 2 * (halves + h))

            front(0, None, 2)
            for a in range(G):
                diagonal(a)
                if a == 0:
                    pair(0, 1, False)
                if a < G - 2:
                    with pe.Fori(max(a + 1, 2), G - 1) as b:
                        pair(a, b, False)
                if a < G - 1:
                    pair(a, G - 1, True)

            pe.wait_ge(prob_ready, G * NB)
            pe.wait_ge(turned_copied, G * (G - 1) * 2)

            def add_neighbours(slot, q, blocks, tails):
                for jb in blocks:
                    lhsT = mgroup[:, slot, jb * GW + q * P:jb * GW + (q + 1) * P]
                    pe.matmul(agg_ps(q, D + 1), lhsT, x1_hi_of(jb // GB)[:, jb % GB, 0:D + 1], start=(jb == 0), stop=False)
                    ins = pe.matmul(agg_ps(q, D), lhsT, x1_lo_of(jb // GB)[:, jb % GB, :], start=False, stop=(jb == NB - 1))
                    if jb in tails:
                        tails[jb]()
                return ins

            def first_group():
                pe.wait_ge(mgroup_loaded[0], 16)
                for sources in (range(0, G - 2), range(G - 2, G - 1), range(G - 1, G)):
                    for g in sources:
                        pe.wait_ge(x1_ready, (g + 1) * GB)
                        pe.wait_ge(x1_ones_ready, g + 1)
                    for q in range(GB):
                        ins = add_neighbours(0, q, range(sources.start * GB, sources.stop * GB), {})
                        if sources.stop == G:
                            ins.then_inc(agg_done, 1)
                pe.wait_ge(attn_copied, NB)

            def aggregate(pair, b, ig, q, slot, tails):
                if q == 0:
                    pe.wait_ge(mgroup_loaded[slot], pair * 16 + 16)
                wait_apart(pe, agg_ready, b - GB + 1, pe_passed)
                add_neighbours(slot, q, range(NB), tails).then_inc(agg_done, 1)

            def turn(b, ig, q):
                pe.wait_ge(agg_ready, b + 1)
                pe.wait_ge(xb_loaded[q], (ig + 1) * 16)
                wait(pe, tr_ready, b - 1)
                slot = q % 2
                for k in range(KD):
                    pe.transpose(tr_ps(slot)[:, k * P:(k + 1) * P], xres[:, q, k * P:(k + 1) * P], ident[:, :])
                for k in range(KD):
                    ins = pe.transpose(tr_ps(slot)[:, (KD + k) * P:(KD + k + 1) * P], agg[:, slot, k * P:(k + 1) * P], ident[:, :])
                ins.then_inc(tr_done, 1)

            def dense(b, ig, q):
                pe.wait_ge(tr_ready, b + 1)
                wait(pe, dense_read, b - 1)
                for k in range(2 * KD):
                    ins = pe.matmul(dense_ps(q % 2), trT[:, q % 2, k, :], mixw[:, k, :], start=(k == 0), stop=(k == 2 * KD - 1))
                ins.then_inc(dense_done, 1)

            def spread(*blocks):
                work = [lambda part=part, block=block: part(*block) for block in blocks for part in (turn, dense)]
                return {6 + n * (NB - 8) // len(work): piece for n, piece in enumerate(work)}

            def layer1_pair(pair, first):
                for half in range(2):
                    ig = pair * 2 + half
                    if first and half == 0:
                        first_group()
                        continue
                    for q in range(GB):
                        b = ig * GB + q
                        if first and q == 0:
                            tails = spread((0, 0, 0), (1, 0, 1), (2, 0, 2))
                        elif first and q == 1:
                            tails = spread((3, 0, 3), (4, 1, 0))
                        else:
                            before = (b - 1, ig, q - 1) if q else (b - 1, ig - 1, GB - 1)
                            tails = spread(before)
                        aggregate(pair, b, ig, q, half, tails)

            layer1_pair(0, True)
            with pe.Fori(1, NPAIR) as pair:
                layer1_pair(pair, False)
            turn(NB - 1, G - 1, GB - 1)
            dense(NB - 1, G - 1, GB - 1)


def kernel(x, adj, L0_gnn_W, L1_gnn_W_self, L1_gnn_b_self, L1_gnn_W_nb, L1_gnn_b_nb, L1_gnn_W_comb, L1_gnn_b_comb):
    import numpy as np
    import concourse.bacc as bacc
    from concourse.bass_utils import run_bass_kernel_spmd

    arrays = {
        "xT": np.ascontiguousarray(np.asarray(x).T),
        "x": np.ascontiguousarray(np.asarray(x)),
        "adjT": np.ascontiguousarray(np.asarray(adj).T),
        "w0T": np.ascontiguousarray(np.asarray(L0_gnn_W).T),
        "w_selfT": np.ascontiguousarray(np.asarray(L1_gnn_W_self).T),
        "b_self": np.ascontiguousarray(np.asarray(L1_gnn_b_self)),
        "w_nbT": np.ascontiguousarray(np.asarray(L1_gnn_W_nb).T),
        "b_nb": np.ascontiguousarray(np.asarray(L1_gnn_b_nb)),
        "w_comb": np.ascontiguousarray(np.asarray(L1_gnn_W_comb)),
        "b_comb": np.ascontiguousarray(np.asarray(L1_gnn_b_comb)),
    }
    nc = bacc.Bacc("TRN2", target_bir_lowering=False, num_devices=1)
    args = [nc.dram_tensor(name, a.shape, mybir.dt.from_np(a.dtype), kind="ExternalInput").ap()
            for name, a in arrays.items()]
    out = nc.dram_tensor("out", (N, D), F32, kind="ExternalOutput").ap()
    gnn_program(nc, *args, out)
    r = run_bass_kernel_spmd(nc, [arrays], core_ids=[0])
    return r.results[0]["out"]
```
